# Optimizing a Trainium2 kernel written in Bass

```python
import numpy as np
import jax
import jax.numpy as jnp

def _softmax(x, axis=-1):
    return jax.nn.softmax(x, axis=axis)

def _gelu(x):
    return jax.nn.gelu(x, approximate=True)

def _silu(x):
    return jax.nn.silu(x)

def _sigmoid(x):
    return jax.nn.sigmoid(x)

def _layernorm(x, axis=-1, eps=1e-05):
    m = jnp.mean(x, axis=axis, keepdims=True)
    v = jnp.var(x, axis=axis, keepdims=True)
    return (x - m) / jnp.sqrt(v + eps)

def _scatter_add(tgt, idx, src, axis=0):
    return tgt.at[idx].add(src)

def _segment_sum(src, seg, n):
    return jax.ops.segment_sum(src, seg, n)
kernel_name = 'mk_seq_postln_d1_jaxref_r4_0fdc2e'

def setup_inputs(seed: int=0):
    np.random.seed(seed)
    _w = jnp.asarray

    def _L0_attn_setup():
        import jax, jax.numpy as jnp
        import numpy as np
        LN_EPS = 1e-05

        def _phi(x):
            return jax.nn.elu(x) + 1.0
        key = jax.random.key(seed)
        ks = jax.random.split(key, 5)
        B, N, D = (4, 2048, 256)
        s = 1.0 / np.sqrt(D)
        return {'H': jax.random.normal(ks[0], (B, N, D), dtype=jnp.float32), 'W_qkv': jax.random.normal(ks[1], (3 * D, D), dtype=jnp.float32) * s, 'b_qkv': jax.random.normal(ks[2], (3 * D,), dtype=jnp.float32) * 0.01, 'W_proj': jax.random.normal(ks[3], (D, D), dtype=jnp.float32) * s, 'b_proj': jax.random.normal(ks[4], (D,), dtype=jnp.float32) * 0.01, 'gamma': jnp.ones((D,), dtype=jnp.float32), 'beta': jnp.zeros((D,), dtype=jnp.float32)}
    _L0_attn_in = _L0_attn_setup()

    def _L0_ffn_setup():
        import jax, jax.numpy as jnp
        import numpy as np
        B, S, H = (4, 512, 256)
        E = 8
        GS = 2
        NG = E // GS
        F = int(H * 4 * (2.0 / 3.0))
        key = jax.random.key(seed)
        ks = jax.random.split(key, 7)
        sc_h = 1.0 / np.sqrt(H)
        sc_f = 1.0 / np.sqrt(F)
        return {'x': jax.random.normal(ks[0], (B, S, H), dtype=jnp.float32), 'Wr': jax.random.normal(ks[1], (H, E), dtype=jnp.float32) * sc_h, 'br': jnp.zeros((E,), dtype=jnp.float32), 'W_up': jax.random.normal(ks[2], (NG, H, F), dtype=jnp.float32) * sc_h, 'b_up': jax.random.normal(ks[3], (NG, F), dtype=jnp.float32) * 0.01, 'W_down': jax.random.normal(ks[4], (E, F, H), dtype=jnp.float32) * sc_f, 'b_down': jax.random.normal(ks[5], (E, H), dtype=jnp.float32) * 0.01}
    _L0_ffn_in = _L0_ffn_setup()
    _d = {'L0_attn_H': _L0_attn_in['H'], 'L0_attn_W_qkv': _L0_attn_in['W_qkv'], 'L0_attn_b_qkv': _L0_attn_in['b_qkv'], 'L0_attn_W_proj': _L0_attn_in['W_proj'], 'L0_attn_b_proj': _L0_attn_in['b_proj'], 'L0_attn_gamma': _L0_attn_in['gamma'], 'L0_attn_beta': _L0_attn_in['beta'], 'L0_ffn_Wr': _L0_ffn_in['Wr'], 'L0_ffn_br': _L0_ffn_in['br'], 'L0_ffn_W_up': _L0_ffn_in['W_up'], 'L0_ffn_b_up': _L0_ffn_in['b_up'], 'L0_ffn_W_down': _L0_ffn_in['W_down'], 'L0_ffn_b_down': _L0_ffn_in['b_down']}
    _x0 = _d['L0_attn_H']
    _d['L0_attn_H'] = jax.random.normal(jax.random.fold_in(jax.random.key(seed), 1), (1, 4096, 256), dtype=_x0.dtype)
    del _x0
    return _d

def reference(L0_attn_H, L0_attn_W_qkv, L0_attn_b_qkv, L0_attn_W_proj, L0_attn_b_proj, L0_attn_gamma, L0_attn_beta, L0_ffn_Wr, L0_ffn_br, L0_ffn_W_up, L0_ffn_b_up, L0_ffn_W_down, L0_ffn_b_down):

    def _L0_attn_ref(H, W_qkv, b_qkv, W_proj, b_proj, gamma, beta):
        import jax, jax.numpy as jnp
        import numpy as np
        LN_EPS = 1e-05

        def _phi(x):
            return jax.nn.elu(x) + 1.0
        B, N, D = H.shape
        num_heads = 16
        head_dim = D // num_heads
        residual = H
        qkv = jnp.einsum('bnd,ed->bne', H, W_qkv) + b_qkv
        qkv = qkv.reshape(B, N, 3, num_heads, head_dim).transpose(2, 0, 3, 1, 4)
        q, k, v = (qkv[0], qkv[1], qkv[2])
        q = _phi(q)
        k = _phi(k)
        kv = jnp.einsum('bhnd,bhnv->bhdv', k, v)
        k1 = k.sum(axis=2)
        qkv_out = jnp.einsum('bhnd,bhdv->bhnv', q, kv)
        qk1 = jnp.sum(q * k1[:, :, None, :], axis=-1, keepdims=True)
        out = qkv_out / jnp.clip(qk1, 1e-06, None)
        out = out.reshape(B, N, D)
        out = jnp.einsum('bnd,ed->bne', out, W_proj) + b_proj
        mu = out.mean(axis=-1, keepdims=True)
        var = out.var(axis=-1, keepdims=True)
        out = (out - mu) * jax.lax.rsqrt(var + LN_EPS) * gamma + beta
        return out + residual

    def _L0_ffn_ref(x, Wr, br, W_up, b_up, W_down, b_down):
        import jax, jax.numpy as jnp
        import numpy as np
        B, S, H = (4, 512, 256)
        E = 8
        GS = 2
        NG = E // GS
        F = int(H * 4 * (2.0 / 3.0))
        b, s, h = x.shape
        n_tok = b * s
        k = n_tok // E
        xf = x.reshape(n_tok, h)
        logits = xf @ Wr + br
        Sm = jax.nn.softmax(logits, axis=-1)
        G_t, idx_t = jax.lax.top_k(Sm.T, k)
        G = G_t.T
        idx = idx_t.T
        tokens = xf[idx]
        group = jnp.arange(E) // GS
        Wu = W_up[group]
        bu = b_up[group]
        mid = jax.nn.silu(jnp.einsum('keh,ehf->kef', tokens, Wu) + bu)
        out = jnp.einsum('kef,efh->keh', mid, W_down) + b_down
        y = jnp.zeros_like(xf).at[idx].add(G[..., None] * out)
        return y.reshape(b, s, h)
    x = L0_attn_H
    x = _layernorm(x + _L0_attn_ref(x, L0_attn_W_qkv, L0_attn_b_qkv, L0_attn_W_proj, L0_attn_b_proj, L0_attn_gamma, L0_attn_beta), axis=-1)
    x = _layernorm(x + _L0_ffn_ref(x, L0_ffn_Wr, L0_ffn_br, L0_ffn_W_up, L0_ffn_b_up, L0_ffn_W_down, L0_ffn_b_down), axis=-1)
    return x

_drawn_inputs = setup_inputs


def setup_inputs(seed=0):
    import zlib

    import numpy as np

    out = dict(_drawn_inputs(seed))
    spreads = {'L0_attn_gamma': (1.0, 0.2), 'L0_attn_beta': (0.0, 0.1), 'L0_ffn_br': (0.0, 0.1)}
    factors = {'L0_ffn_b_up': 25.214, 'L0_ffn_b_down': 8.0}
    for name, (base, spread) in spreads.items():
        noise = np.random.default_rng([zlib.crc32(name.encode()), seed]).standard_normal(out[name].shape)
        drawn = base * np.exp(spread * noise) if base else spread * noise
        out[name] = jnp.asarray(drawn.astype(out[name].dtype))
    for name, factor in factors.items():
        out[name] = (out[name] * factor).astype(out[name].dtype)
    return out
```

```python
from contextlib import ExitStack

import numpy as np

import concourse.bass as bass
from concourse import mybir

P = 128
ALU = mybir.AluOpType
ACT = mybir.ActivationFunctionType
AX = mybir.AxisListType
F32 = mybir.dt.float32
BF16 = mybir.dt.bfloat16
I32 = mybir.dt.int32

N = 4096
D = 256
C = D // P
HEADS = 16
HD = D // HEADS
HH = HEADS // C
TB = 4
BLK = TB * P
NT = N // P
NB = NT // TB
E = 8
GS = 2
G = E // GS
F = int(D * 4 * (2.0 / 3.0))
FT = -(-F // P)
FR = F - (FT - 1) * P
KSEL = N // E
KT = KSEL // P
EPS = 1e-5
ROW = D + E
HC = D + 2
CH = 2 * P
NCH = N // CH
BITS = 30
RB = 2
ROUNDS = BITS // RB
CAND = (1 << RB) - 1

C_ID, C_HEAD, C_SAME, C_BEFORE, C_IOTA = (P * i for i in range(5))
C_HEAD8 = 5 * P
C_FOUR = C_HEAD8 + HH
C_TILE = C_FOUR + KT
C_PART = C_TILE + NT
C_HALF = C_PART + 1
C_EPS = C_HALF + TB
C_NEG = C_EPS + TB
C_ALL = C_NEG + TB
R_BK, R_BP, R_GAMMA, R_BETA = (D * i for i in range(4))
R_BR = 4 * D
R_ALL = R_BR + E
PER = N // 2 // P
HALF = PER // TB


def constants():
    p = np.arange(P)
    c = np.zeros((P, C_ALL), np.float32)
    c[:, C_ID:C_ID + P] = np.eye(P)
    c[:, C_HEAD:C_HEAD + P] = p[:, None] // HD == p // HD
    c[:, C_SAME:C_SAME + P] = p[:, None] % E == p % E
    c[:, C_BEFORE:C_BEFORE + P] = (p[:, None] % E == p % E) & (p[:, None] < p)
    c[:, C_IOTA:C_IOTA + P] = p
    c[:, C_HEAD8:C_HEAD8 + HH] = p[:, None] // HD == np.arange(HH)
    c[:, C_FOUR:C_FOUR + KT] = np.arange(KT)
    c[:, C_TILE:C_TILE + NT] = np.arange(NT)
    c[:, C_PART] = p
    c[:, C_HALF:C_HALF + TB] = -0.5
    c[:, C_EPS:C_EPS + TB] = EPS
    c[:, C_NEG:C_NEG + TB] = -1.0
    steps = [j << (BITS - RB * (r + 1)) for r in range(ROUNDS) for j in range(1, CAND + 1)]
    return c, np.tile(np.array(steps, np.int32), (P, 1))


def build(nc, x, xt, xtq, wqkv, bq, bv, wp, rows, wr, wup, bup, wdn, cst, steps, out):
    with ExitStack() as ctx:
        def sb(name, shape, dt=F32):
            return ctx.enter_context(nc.sbuf_tensor(name, shape, dt))

        def sem(name):
            return ctx.enter_context(nc.semaphore(name))

        table = nc.dram_tensor("table", [N, ROW], F32, kind="Internal").ap()
        ysum = nc.dram_tensor("ysum", [N, D], F32, kind="Internal").ap()

        ps = ctx.enter_context(nc.psum_tensor("ps", [P, 8, 512], F32))

        cs = sb("cs", [P, C_ALL])
        stp = sb("stp", [P, ROUNDS * CAND], I32)
        rw = sb("rw", [P, R_ALL])
        wqkv_s = sb("wqkv_s", [P, C, 3 * D])
        wp_s = sb("wp_s", [P, C, D])
        wr_s = sb("wr_s", [P, C, E])
        bq_s = sb("bq_s", [P, C])
        bv_s = sb("bv_s", [1, D])
        bup_s = sb("bup_s", [P, G, FT])
        h_all = sb("h_all", [P, NT, HC])
        ht_all = sb("ht_all", [P, C, N])
        heads = sb("heads", [P, NT, D])
        early = heads[:].rearrange("p t d -> p (t d)")
        ht_ring = early[:, 0:2 * C * BLK].rearrange("p (a c n) -> p a c n", a=2, c=C)
        kx, kneg, kexp = (early[:, at * D:(at + 4) * D].rearrange("p (a d) -> p a d", a=2) for at in (8, 12, 16))
        key = early[:, 20 * D:28 * D].rearrange("p (a u d) -> p a u d", a=4, u=2)
        kh = sb("kh", [P, C, HC])
        kht = sb("kht", [P, C, D])
        k1row = sb("k1row", [1, D])
        kvk = sb("kvk", [P, C, P + HH])
        qrel = sb("qrel", [P, C, BLK])
        qexp = sb("qexp", [P, C, BLK])
        qt = sb("qt", [P, C, BLK])
        den = sb("den", [P, TB, HEADS])
        rden = sb("rden", [P, TB, HEADS])
        att = sb("att", [P, TB, D])
        att_t = sb("att_t", [P, TB, C, P])
        zb = sb("zb", [P, TB, D])
        zn = sb("zn", [P, 2, D])
        st = sb("st", [P, 2, 6])
        mv = sb("mv", [P, TB, 2])
        mv2 = sb("mv2", [P, TB, 2])
        ve = sb("ve", [P, TB])
        ve2 = sb("ve2", [P, TB])
        rstd = sb("rstd", [P, TB])
        rstd2 = sb("rstd2", [P, TB])
        xx = sb("xx", [P, 2, D])
        xb = sb("xb", [P, TB, D])
        us = sb("us", [P, TB, D])
        x1 = sb("x1", [P, TB, D])
        x1t = sb("x1t", [P, TB, C, P])
        lg = sb("lg", [P, NT, E])
        mx = sb("mx", [P, NT])
        sm = sb("sm", [P, NT])
        prob = sb("prob", [P, NT, E])
        sv = sb("sv", [P, CH])
        cand = sb("cand", [P, CAND], I32)
        thr = sb("thr", [P, 1 + CAND])
        cnt = sb("cnt", [P, CAND])
        junk = sb("junk", [P, CAND, CH])
        chosen = sb("chosen", [P, CH])
        place = sb("place", [P, CH])
        above = sb("above", [P, CH])
        equal = sb("equal", [P, CH])
        scan = sb("scan", [P, CH])
        ends = sb("ends", [P, 4])
        need = sb("need", [P, 1])
        slot_i = sb("slot_i", [P, CH], I32)
        part_i = sb("part_i", [P, CH], I32)
        part_f = sb("part_f", [P, CH])
        four_i = sb("four_i", [P, CH], I32)
        four_f = sb("four_f", [P, CH])
        dead = ht_all[:].rearrange("p c n -> p (c n)")
        mid = dead[:, 0:FT * KSEL].rearrange("p (f k) -> p f k", f=FT)
        hot = dead[:, FT * KSEL:FT * KSEL + NT * P // 2].bitcast(BF16).rearrange("p (s k) -> p s k", s=NT)
        eq4 = sb("eq4", [P, NT, KT])
        pay = sb("pay", [P, NT, 2, KT], BF16)
        idp = sb("idp", [P, 2 * KT])
        idx = sb("idx", [P, 2, KT], I32)
        idx_add = sb("idx_add", [P, KT], I32)
        gate = sb("gate", [P, 2, KT])
        wup_s = sb("wup_s", [P, C, F])
        wdn_s = sb("wdn_s", [P, FT, D])
        xg = sb("xg", [P, KT, ROW])
        xgt = sb("xgt", [P, C, KSEL])
        yb = sb("yb", [P, KT, D])
        fst = sb("fst", [P, 2, 6])
        fmv = sb("fmv", [P, 2, TB, 2])
        fve = sb("fve", [P, 2, TB])
        frs = sb("frs", [P, 2, TB])
        fnm = sb("fnm", [P, 2, TB])

        s_stood = sem("s_stood")
        s_keyw = sem("s_keyw")
        s_wts = sem("s_wts")
        s_ring = [sem(f"s_ring{i}") for i in range(2)]
        s_h = [sem(f"s_h{i}") for i in range(2)]
        s_ht = [sem(f"s_ht{i}") for i in range(2)]
        s_ones = sem("s_ones")
        s_kmm = sem("s_kmm")
        s_kx = sem("s_kx")
        s_kneg = sem("s_kneg")
        s_kexp = sem("s_kexp")
        s_key = sem("s_key")
        s_khmm = sem("s_khmm")
        s_kh = sem("s_kh")
        s_khtmm = sem("s_khtmm")
        s_kht = sem("s_kht")
        s_kvmm = sem("s_kvmm")
        s_kv = sem("s_kv")
        s_qmm = sem("s_qmm")
        s_qact = sem("s_qact")
        s_qread = sem("s_qread")
        s_q = sem("s_q")
        s_amm = sem("s_amm")
        s_den = sem("s_den")
        s_att = sem("s_att")
        s_attin = [sem(f"s_attin{i}") for i in range(2)]
        s_attmm = sem("s_attmm")
        s_attt = sem("s_attt")
        s_zmm = sem("s_zmm")
        s_zb = sem("s_zb")
        s_st = sem("s_st")
        s_st2 = sem("s_st2")
        s_mv = sem("s_mv")
        s_ve = sem("s_ve")
        s_rs = sem("s_rs")
        s_xx = sem("s_xx")
        s_xb = sem("s_xb")
        s_zn = sem("s_zn")
        s_us = sem("s_us")
        s_mv2 = sem("s_mv2")
        s_ve2 = sem("s_ve2")
        s_rs2 = sem("s_rs2")
        s_x1 = sem("s_x1")
        s_x1out = sem("s_x1out")
        s_x1free = sem("s_x1free")
        s_x1mm = sem("s_x1mm")
        s_x1t = sem("s_x1t")
        s_lmm = sem("s_lmm")
        s_lg = sem("s_lg")
        s_soft = sem("s_soft")
        s_exp = sem("s_exp")
        s_prob = sem("s_prob")
        s_probout = sem("s_probout")
        s_svmm = sem("s_svmm")
        s_thr = sem("s_thr")
        s_kept = sem("s_kept")
        s_cand = sem("s_cand")
        s_cnt = sem("s_cnt")
        s_tot = sem("s_tot")
        s_sel = sem("s_sel")
        s_pick = sem("s_pick")
        s_pickmm = sem("s_pickmm")
        s_slot = sem("s_slot")
        s_wup = sem("s_wup")
        s_wdn = sem("s_wdn")
        s_eq4 = sem("s_eq4")
        s_hot = sem("s_hot")
        s_idmm = sem("s_idmm")
        s_idp = sem("s_idp")
        s_idx = sem("s_idx")
        s_gat = sem("s_gat")
        s_gate = sem("s_gate")
        s_xtmm = sem("s_xtmm")
        s_xt = sem("s_xt")
        s_umm = sem("s_umm")
        s_mid = sem("s_mid")
        s_midone = sem("s_midone")
        s_dmm = sem("s_dmm")
        s_y = sem("s_y")
        s_idadd = sem("s_idadd")
        s_add = sem("s_add")
        s_ybfree = sem("s_ybfree")
        s_yin = [sem(f"s_yin{i}") for i in range(2)]
        s_fst = sem("s_fst")
        s_fmv = sem("s_fmv")
        s_fve = sem("s_fve")
        s_frs = sem("s_frs")
        s_fnm = sem("s_fnm")
        s_fin = sem("s_fin")
        s_out = [sem(f"s_out{i}") for i in range(2)]

        ident = cs[:, C_ID:C_ID + P]
        table_t = table.rearrange("(s p) c -> p s c", p=P)
        ysum_t = ysum.rearrange("(s p) c -> p s c", p=P)
        out_t = out.rearrange("(s p) c -> p s c", p=P)
        x_t = x.rearrange("(s p) c -> p s c", p=P)
        xt_t = xt.rearrange("(c p) n -> p c n", p=P)
        xtq_t = xtq.rearrange("(c p) n -> p c n", p=P)

        block = ctx.enter_context(nc.Block())

        def pair_steps(eng, step):
            for j in range(4):
                step(0, j, "first")
            with eng.Fori(1, NB // 2 - 1) as i:
                for j in range(4):
                    step(i, j, "loop")
            for j in range(4):
                step(NB // 2 - 1, j, "last")
            for j in range(2):
                step(NB // 2, j, "drain")

        def tile_steps(eng, step):
            for kind, begin, end in (("attend", 0, HALF), ("begin", HALF, HALF + 1), ("both", HALF + 1, NB - 1),
                                     ("attended", NB - 1, NB), ("rows", NB, NB + HALF - 1),
                                     ("last", NB + HALF - 1, NB + HALF), ("drain", NB + HALF, NB + HALF + 1)):
                if end - begin == 1:
                    for t in range(TB):
                        step(begin, t, kind)
                else:
                    with eng.Fori(begin, end) as n:
                        for t in range(TB):
                            step(n, t, kind)

        def attends(kind):
            return kind in ("attend", "begin", "both", "attended")

        def prefetches(kind):
            return kind in ("attend", "begin", "both")

        def has_row(kind, t, lag):
            return {"attend": False, "begin": t >= lag, "drain": t < lag}.get(kind, True)

        def stand(eng, semaphore, value):
            eng.wait_ge(semaphore, value)
            eng.sem_inc(s_stood, 1)

        def has(kind, t, lag):
            return {"first": t >= lag, "drain": t < lag}.get(kind, True)

        @block.sync
        def _(sp):
            sp.dma_start(wqkv_s[:, :, D:2 * D], wqkv.rearrange("(c p) e -> p c e", p=P)[:, :, D:2 * D]).then_inc(s_keyw, 16)
            sp.dma_start(rw[:], rows).then_inc(s_keyw, 16)
            def load_block(i, half):
                b = 2 * i + half
                cols = bass.ds(b * BLK, BLK)
                sp.dma_start(ht_ring[:, half], xt_t[:, :, cols]).then_inc(s_ring[half], 16)
                sp.dma_start(h_all[:, bass.ds(b * TB, TB), 0:D], x_t[:, bass.ds(b * TB, TB), :]).then_inc(s_h[half], 16)

            load_block(0, 0)
            load_block(0, 1)
            sp.dma_start(cs[:], cst).then_inc(s_wts, 16)
            sp.dma_start(stp[:], steps).then_inc(s_wts, 16)
            for half in (0, 1):
                sp.dma_start(wqkv_s[:, :, 2 * D * half:2 * D * half + D],
                             wqkv.rearrange("(c p) e -> p c e", p=P)[:, :, 2 * D * half:2 * D * half + D]).then_inc(s_wts, 16)
            sp.dma_start(wp_s[:], wp.rearrange("(c p) e -> p c e", p=P)).then_inc(s_wts, 16)
            sp.dma_start(wr_s[:], wr.rearrange("(c p) e -> p c e", p=P)).then_inc(s_wts, 16)
            sp.dma_start(bq_s[:], bq).then_inc(s_wts, 16)
            sp.dma_start(bv_s[:], bv).then_inc(s_wts, 16)
            sp.dma_start(bup_s[:], bup).then_inc(s_wts, 16)
            with sp.Fori(1, NB // 2) as i:
                for half in range(2):
                    stand(sp, s_kmm, 4 * i + (2 * half - 2))
                    stand(sp, s_h[half], 16 * i)
                    load_block(i, half)
            with sp.Fori(0, NB // 2) as i:
                for half in range(2):
                    cols = bass.ds((2 * i + half) * BLK, BLK)
                    sp.dma_start(ht_all[:, :, cols], xtq_t[:, :, cols]).then_inc(s_ht[half], 16)
                    stand(sp, s_ht[half], 16 * i + 16)

            def load_up(g):
                sp.dma_start(wup_s[:], wup[bass.ds(g, 1)].rearrange("g (c p) f -> p (g c) f", p=P)).then_inc(s_wup, 16)

            def load_down(e):
                full = (FT - 1) * P
                sp.dma_start(wdn_s[:, 0:FT - 1, :],
                             wdn[bass.ds(e, 1), 0:full, :].rearrange("g (f p) d -> p (g f) d", p=P)).then_inc(s_wdn, 16)
                sp.dma_start(wdn_s[0:FR + 1, FT - 1:FT, :],
                             wdn[bass.ds(e, 1), full:F + 1, :].rearrange("g p d -> p g d")).then_inc(s_wdn, 16)

            load_up(0)
            load_down(0)

            def store_tile(n, t):
                stand(sp, s_x1, TB * n + (t + 1))
                tile = TB * n + t
                sp.dma_start(table_t[:, bass.ds(tile, 1), 0:D], x1[:, t:t + 1, :]).then_inc(s_x1out, 16)
                sp.dma_start(ysum_t[:, bass.ds(tile, 1), :], x1[:, t:t + 1, :]).then_inc(s_x1out, 16)
                stand(sp, s_x1out, 32 * TB * n + 32 * (t + 1))
                sp.sem_inc(s_x1free, 1)

            sp.sem_inc(s_x1free, TB)
            with sp.Fori(0, NB) as n:
                for t in range(TB):
                    store_tile(n, t)
            sp.wait_ge(s_prob, 1)
            with nc.allow_non_contiguous_dma(reason="eight probabilities a token"):
                sp.dma_start(table_t[:, :, D:ROW], prob[:]).then_inc(s_probout, 16)
            for e in range(1, GS):
                sp.wait_ge(s_dmm, KT * e)
                load_down(e)
            with sp.Fori(1, G) as g:
                stand(sp, s_umm, GS * FT * g)
                load_up(g)
                for k in range(GS):
                    stand(sp, s_dmm, GS * KT * g + KT * k)
                    load_down(GS * g + k)
            sp.wait_ge(s_ybfree, E + 1)
            with sp.Fori(0, NB // 2) as i:
                for half in range(2):
                    tiles = bass.ds((2 * i + half) * TB, TB)
                    sp.dma_start(h_all[:, tiles, 0:D], ysum_t[:, tiles, :]).then_inc(s_yin[half], 16)
                    stand(sp, s_yin[half], 16 * i + 16)
            with sp.Fori(0, NB // 2) as i:
                for half in range(2):
                    b = 2 * i + half
                    tiles = bass.ds(b * TB, TB)
                    stand(sp, s_fin, TB * b + 3 * TB)
                    sp.dma_start(out_t[:, tiles, :], h_all[:, tiles, 0:D]).then_inc(s_out[half], 16)
                    stand(sp, s_out[half], 16 * i + 16)

        @block.tensor
        def _(pe):
            def keys(i, j, kind):
                bank = j % 2
                if has(kind, j, 0):
                    if j % 2 == 0:
                        pe.wait_ge(s_ring[j // 2], 16 * i + 16)
                    pe.wait_ge(s_kx, 4 * i + (j + 1))
                    for u in range(2):
                        for c in range(C):
                            at = (2 * (j % 2) + u) * P
                            mm = pe.matmul(ps[:, bank, u * D:(u + 1) * D], ht_ring[:, j // 2, c, at:at + P],
                                           wqkv_s[:, c, D:2 * D], start=(c == 0), stop=(c == C - 1))
                    mm.then_inc(s_kmm, 1)
                if has(kind, j, 2):
                    back = j - 2
                    pe.wait_ge(s_key, 4 * i + (back + 1))
                    if j % 2 == 0:
                        if j == 0:
                            pe.wait_ge(s_h[1], 16 * i)
                        else:
                            pe.wait_ge(s_h[0], 16 * i + 16)
                    for u in range(2):
                        for c in range(C):
                            begins = kind == "first" and back == 0 and u == 0
                            ends_ = kind == "drain" and j == 1 and u == 1
                            mm = pe.matmul(ps[:, 2 + c, 0:HC], key[:, back % 4, u, c * P:(c + 1) * P],
                                           h_all[:, bass.ds(i * 8 + (2 * back + u), 1), :].rearrange("p a h -> p (a h)"),
                                           start=begins, stop=ends_, skip_group_check=True)
                    mm.then_inc(s_khmm, 1)

            pe.wait_ge(s_keyw, 32)
            pe.wait_ge(s_ones, 1)
            pair_steps(pe, keys)

            pe.wait_ge(s_wts, 16 * 9)
            pe.wait_ge(s_kh, 2)
            for c in range(C):
                for h in range(C):
                    pe.transpose(ps[:, 4, h * D + c * P:h * D + (c + 1) * P], kh[:, c, h * P:(h + 1) * P], ident)
            for c in range(C):
                mm = pe.transpose(ps[0:1, 5, c * P:(c + 1) * P], kh[:, c, D:D + 1], ident)
            mm.then_inc(s_khtmm, 1)
            pe.wait_ge(s_kht, 2)
            for c in range(C):
                half = slice(c * P, (c + 1) * P)
                for h in range(C):
                    pe.matmul(ps[:, 6, half], kht[:, h, half], wqkv_s[:, h, 2 * D + c * P:2 * D + (c + 1) * P],
                              start=(h == 0), stop=False)
                mm = pe.matmul(ps[:, 6, half], k1row[:, half], bv_s[:, half], start=False, stop=True)
            mm.then_inc(s_kvmm, 1)

            pe.wait_ge(s_ht[0], 16 * (NB // 2))
            pe.wait_ge(s_ht[1], 16 * (NB // 2))

            def queries(n, m):
                for c in range(C):
                    mm = pe.matmul(ps[:, m, :], wqkv_s[:, c, m * P:(m + 1) * P], ht_all[:, c, bass.ds(n * BLK, BLK)],
                                   start=(c == 0), stop=(c == C - 1))
                mm.then_inc(s_qmm, 1)

            def tokens(n, t, kind):
                row = TB * (n - HALF) + t
                if attends(kind):
                    if t == 0:
                        pe.wait_ge(s_q, C * n + C)
                    pe.wait_ge(s_att, TB * n + (t + 1))
                    for c in range(C):
                        mm = pe.matmul(ps[:, 2 + t % 2, c * (P + HH):(c + 1) * (P + HH)], qt[:, c, t * P:(t + 1) * P],
                                       kvk[:, c, :], start=True, stop=True)
                    mm.then_inc(s_amm, 1)
                if has_row(kind, t, 1):
                    pe.wait_ge(s_attt, row)
                    pe.wait_ge(s_zb, row)
                    for c in range(C):
                        mm = pe.matmul(ps[:, 5 + (t - 1) % 2, 0:D], att_t[:, (t - 1) % TB, c, :], wp_s[:, c, :],
                                       start=(c == 0), stop=(c == C - 1))
                    mm.then_inc(s_zmm, 1)
                if has_row(kind, t, 4):
                    pe.wait_ge(s_x1t, row - 3)
                    for c in range(C):
                        mm = pe.matmul(ps[:, 7, D:D + E], x1t[:, t, c, :], wr_s[:, c, :], start=(c == 0), stop=(c == C - 1))
                    mm.then_inc(s_lmm, 1)
                if prefetches(kind) and t < C:
                    pe.wait_ge(s_qread, C * n + (t + 1))
                    queries(n + 1, t)
                if has_row(kind, t, 0):
                    pe.wait_ge(s_attin[t % 2], 32 * (n - HALF) + 16 * (t // 2 + 1))
                    for c in range(C):
                        mm = pe.transpose(ps[:, 4, c * P:(c + 1) * P], att[:, t, c * P:(c + 1) * P], ident)
                    mm.then_inc(s_attmm, 1)
                if has_row(kind, t, 3):
                    pe.wait_ge(s_x1, row - 2)
                    if has_row(kind, t, 4):
                        pe.wait_ge(s_lg, row - 3)
                    for c in range(C):
                        mm = pe.transpose(ps[:, 7, c * P:(c + 1) * P], x1[:, (t - 3) % TB, c * P:(c + 1) * P], ident)
                    mm.then_inc(s_x1mm, 1)

            for m in range(C):
                queries(0, m)
            pe.wait_ge(s_kv, 1)
            tile_steps(pe, tokens)

            pe.wait_ge(s_prob, 1)
            for h in range(2):
                mm = pe.transpose(ps[:, 0, h * P:(h + 1) * P], prob[:, h * NCH:(h + 1) * NCH, :].rearrange("p i e -> p (i e)"), ident)
            mm.then_inc(s_svmm, 1)
            with pe.Fori(0, ROUNDS) as r:
                pe.wait_ge(s_cnt, r + 1)
                pe.matmul(ps[:, 1, 0:CAND], cs[:, C_SAME:C_SAME + P], cnt[:], start=True, stop=True).then_inc(s_tot, 1)
            pe.wait_ge(s_sel, 1)
            pe.matmul(ps[:, 1, 0:1], cs[:, C_SAME:C_SAME + P], ends[:, 0:1], start=True, stop=True)
            pe.matmul(ps[:, 1, 1:2], cs[:, C_BEFORE:C_BEFORE + P], scan[:, CH - 1:CH], start=True, stop=True).then_inc(s_tot, 1)
            pe.wait_ge(s_sel, 2)
            pe.matmul(ps[:, 1, 0:1], cs[:, C_BEFORE:C_BEFORE + P], place[:, CH - 1:CH], start=True, stop=True).then_inc(s_tot, 1)
            pe.wait_ge(s_pick, 8)
            for h in range(2):
                mm = pe.transpose(ps[:, 0, h * P:(h + 1) * P], scan[:, h * P:(h + 1) * P], ident)
            mm.then_inc(s_pickmm, 1)

            def lists(e):
                pe.wait_ge(s_hot, e + 1)
                for s in range(NT):
                    mm = pe.matmul(ps[:, 6, 0:2 * KT], hot[:, s, :], pay[:, s].rearrange("p w k -> p (w k)"),
                                   start=(s == 0), stop=(s == NT - 1))
                mm.then_inc(s_idmm, 1)

            def turn(e):
                pe.wait_ge(s_gat, 16 * KT * e + 16 * KT)
                for c in range(C):
                    for k in range(KT):
                        mm = pe.transpose(ps[:, 2 + c, k * P:(k + 1) * P], xg[:, k, c * P:(c + 1) * P], ident)
                mm.then_inc(s_xtmm, 1)

            def expert(g, k, last):
                e = GS * g + k
                if not last:
                    lists(e + 1)
                pe.wait_ge(s_xt, C * e + C)
                if k == 0:
                    pe.wait_ge(s_wup, 16 * g + 16)
                for f in range(FT):
                    width = P if f < FT - 1 else FR
                    pe.wait_ge(s_mid, e * FT + (f + 1))
                    for c in range(C):
                        mm = pe.matmul(ps[0:width, f % 2, :], wup_s[:, c, f * P:f * P + width], xgt[:, c, :],
                                       start=(c == 0), stop=(c == C - 1))
                    mm.then_inc(s_umm, 1)
                if not last:
                    turn(e + 1)
                pe.wait_ge(s_wdn, 32 * e + 32)
                for j in range(KT):
                    pe.wait_ge(s_y, e * KT + (j + 1))
                    for f in range(FT):
                        rows_ = P if f < FT - 1 else FR + 1
                        if j == 0:
                            pe.wait_ge(s_mid, e * FT + (f + 3))
                        mm = pe.matmul(ps[:, 4 + j % 2, 0:D], mid[0:rows_, f, j * P:(j + 1) * P], wdn_s[0:rows_, f, :],
                                       start=(f == 0), stop=(f == FT - 1))
                    mm.then_inc(s_dmm, 1)

            lists(0)
            turn(0)
            pe.wait_ge(s_midone, 1)
            with pe.Fori(0, G - 1) as g:
                for k in range(GS):
                    expert(g, k, False)
            for k in range(GS):
                expert(G - 1, k, k == GS - 1)

        @block.vector
        def _(dve):
            dve.memset(h_all[:, :, D:HC], 1.0).then_inc(s_ones, 1)
            dve.sem_inc(s_kx, 2)

            def keys(i, j, kind):
                if has(kind, j, 0):
                    dve.wait_ge(s_kmm, 4 * i + (j + 1))
                    if kind != "first" or j >= 2:
                        dve.wait_ge(s_key, 4 * i + (j - 1))
                    dve.tensor_tensor(kx[:, j % 2, :].rearrange("p (u d) -> p u d", u=2),
                                      ps[:, j % 2, :].rearrange("p (u d) -> p u d", u=2),
                                      rw[:, R_BK:R_BK + D].unsqueeze(1).to_broadcast([P, 2, D]), ALU.add).then_inc(s_kx, 1)
                if has(kind, j, 1):
                    dve.wait_ge(s_kexp, 4 * i + j)
                    b = (j - 1) % 2
                    dve.scalar_tensor_tensor(out=key[:, (j - 1) % 4].rearrange("p u d -> p (u d)"), in0=kx[:, b, :], scalar=0.0,
                                             in1=kexp[:, b, :], op0=ALU.max, op1=ALU.add).then_inc(s_key, 1)

            dve.wait_ge(s_keyw, 32)
            pair_steps(dve, keys)

            dve.wait_ge(s_khmm, NT // 2)
            for c in range(C):
                dve.tensor_copy(kh[:, c, :], ps[:, 2 + c, 0:HC]).then_inc(s_kh, 1)
            dve.wait_ge(s_kh, 2)
            dve.wait_ge(s_wts, 16 * 9)
            for c in range(C):
                dve.tensor_scalar(kvk[:, c, P:P + HH], cs[:, C_HEAD8:C_HEAD8 + HH], kh[:, c, D:D + 1], None, ALU.mult)
            dve.wait_ge(s_khtmm, 1)
            dve.tensor_copy(kht[:].rearrange("p c d -> p (c d)"), ps[:, 4, :]).then_inc(s_kht, 1)
            dve.tensor_copy(k1row[:], ps[0:1, 5, 0:D]).then_inc(s_kht, 1)
            dve.wait_ge(s_kvmm, 1)
            dve.tensor_tensor(kvk[:, :, 0:P], ps[:, 6, 0:D].rearrange("p (c v) -> p c v", c=C),
                              cs[:, C_HEAD:C_HEAD + P].unsqueeze(1).to_broadcast([P, C, P]), ALU.mult).then_inc(s_kv, 1)

            def make_q(n):
                for m in range(C):
                    dve.wait_ge(s_qread, C * n + (m + 1))
                    dve.scalar_tensor_tensor(out=qt[:, m, :], in0=qexp[:, m, :], scalar=1.0, in1=qrel[:, m, :],
                                             op0=ALU.min, op1=ALU.add).then_inc(s_q, 1)

            def tokens(n, t, kind):
                tile = TB * (n - HALF) + t
                if has_row(kind, t, 2):
                    u = (t - 2) % TB
                    dve.wait_ge(s_rs, tile - 1)
                    dve.tensor_scalar(zn[:, 0, :], zb[:, u, :], mv[:, u, 0:1], rstd[:, u:u + 1],
                                      ALU.subtract, ALU.mult).then_inc(s_zn, 1)
                    dve.wait_ge(s_zn, 2 * tile - 3)
                    dve.tensor_tensor(zn[:, 1, :], zn[:, 0, :], rw[:, R_GAMMA:R_GAMMA + D], ALU.mult).then_inc(s_zn, 1)
                    dve.wait_ge(s_zn, 2 * tile - 2)
                    dve.wait_ge(s_xb, tile - 1)
                    dve.tensor_tensor(us[:, u, :], zn[:, 1, :], xb[:, u, :], ALU.add).then_inc(s_us, 1)
                    dve.wait_ge(s_us, tile - 1)
                    dve.bn_stats(st[:, 1, :], us[:, u, :]).then_inc(s_st2, 1)
                if attends(kind):
                    dve.wait_ge(s_amm, TB * n + (t + 1))
                    bank = ps[:, 2 + t % 2, 0:C * (P + HH)].rearrange("p (c w) -> p c w", c=C)
                    dve.tensor_scalar(den[:, t].rearrange("p (c h) -> p c h", c=C), bank[:, :, P:P + HH], 1e-6, None,
                                      ALU.max).then_inc(s_den, 1)
                    dve.wait_ge(s_den, 2 * TB * n + (2 * t + 1))
                    dve.reciprocal(rden[:, t, :], den[:, t, :]).then_inc(s_den, 1)
                if has_row(kind, t, 2):
                    stand(dve, s_st2, tile - 1)
                    dve.bn_aggr(mv2[:, (t - 2) % TB, :], st[:, 1, :]).then_inc(s_mv2, 1)
                if attends(kind):
                    w = 0 if kind == "attend" else 1
                    j = bass.ds(TB * (n - HALF * w) + t, 1)
                    dve.wait_ge(s_den, 2 * TB * n + (2 * t + 2))
                    dve.tensor_tensor(heads[:, PER * w:PER * (w + 1), :].rearrange("p (c h) (j d) -> p c h j d", c=C, j=PER)[:, :, :, j, :].rearrange("p c h j d -> p c h (j d)"),
                                      bank[:, :, 0:P].rearrange("p c (h d) -> p c h d", h=HH),
                                      rden[:, t, :].rearrange("p (c h) -> p c h", c=C).unsqueeze(3).to_broadcast([P, C, HH, HD]),
                                      ALU.mult).then_inc(s_att, 1)
                if prefetches(kind) and t == TB - 1:
                    make_q(n + 1)
                if has_row(kind, t, 3):
                    u = (t - 3) % TB
                    dve.wait_ge(s_rs2, tile - 2)
                    dve.wait_ge(s_x1free, tile - 2)
                    dve.tensor_scalar(x1[:, u, :], us[:, u, :], mv2[:, u, 0:1], rstd2[:, u:u + 1],
                                      ALU.subtract, ALU.mult).then_inc(s_x1, 1)
                if has_row(kind, t, 4):
                    dve.wait_ge(s_lmm, tile - 3)
                    dve.tensor_tensor(lg[:, bass.ds(tile - 4, 1), :].rearrange("p a e -> p (a e)"), ps[:, 7, D:D + E],
                                      rw[:, R_BR:R_BR + E], ALU.add).then_inc(s_lg, 1)
                if has_row(kind, t, 1):
                    u = (t - 1) % TB
                    dve.wait_ge(s_zmm, tile)
                    dve.tensor_tensor(zb[:, u, :], ps[:, 5 + u % 2, 0:D], rw[:, R_BP:R_BP + D], ALU.add).then_inc(s_zb, 1)
                    dve.wait_ge(s_zb, tile + 2)
                    dve.bn_stats(st[:, 0, :], zb[:, u, :]).then_inc(s_st, 1)
                    stand(dve, s_st, tile)
                    dve.bn_aggr(mv[:, u, :], st[:, 0, :]).then_inc(s_mv, 1)

            dve.sem_inc(s_att, 2)
            dve.sem_inc(s_zb, 2)
            make_q(0)
            tile_steps(dve, tokens)

            wide = [P, NT, E]
            dve.wait_ge(s_lg, NT)
            dve.tensor_reduce(mx[:], lg[:], AX.X, ALU.max).then_inc(s_soft, 1)
            dve.wait_ge(s_soft, 1)
            dve.tensor_tensor(prob[:], lg[:], mx[:].unsqueeze(2).to_broadcast(wide), ALU.subtract).then_inc(s_soft, 1)
            dve.wait_ge(s_exp, 1)
            dve.tensor_reduce(sm[:], lg[:], AX.X, ALU.add).then_inc(s_soft, 1)
            dve.wait_ge(s_soft, 3)
            dve.reciprocal(mx[:], sm[:]).then_inc(s_soft, 1)
            dve.wait_ge(s_soft, 4)
            dve.tensor_tensor(prob[:], lg[:], mx[:].unsqueeze(2).to_broadcast(wide), ALU.mult).then_inc(s_prob, 1)

            dve.memset(thr[:], 0.0).then_inc(s_thr, 1)
            dve.memset(mid[0:64, FT - 1, :], 1.0).then_inc(s_midone, 1)
            dve.wait_ge(s_svmm, 1)
            dve.tensor_copy(sv[:], ps[:, 0, 0:CH]).then_inc(s_cand, 1)
            with dve.Fori(0, ROUNDS) as r:
                dve.wait_ge(s_thr, r + 1)
                dve.tensor_tensor(cand[:], thr[:, 0:1].bitcast(I32).to_broadcast([P, CAND]), stp[:, bass.ds(r * CAND, CAND)],
                                  ALU.bitwise_or).then_inc(s_cand, 1)
                dve.wait_ge(s_cand, r + 2)
                for q in range(CAND):
                    last = dve.tensor_scalar(junk[:, q, :], sv[:], cand[:, q:q + 1].bitcast(F32), 0.0, ALU.is_ge, ALU.add,
                                             accum_out=cnt[:, q:q + 1])
                last.then_inc(s_cnt, 1)
                dve.wait_ge(s_tot, r + 1)
                dve.scalar_tensor_tensor(out=thr[:, 1:1 + CAND], in0=ps[:, 1, 0:CAND], scalar=KSEL - 0.5,
                                         in1=cand[:].bitcast(F32), op0=ALU.is_ge, op1=ALU.mult).then_inc(s_kept, 1)
                dve.wait_ge(s_kept, r + 1)
                dve.tensor_reduce(thr[:, 0:1], thr[:], AX.X, ALU.max).then_inc(s_thr, 1)
            dve.wait_ge(s_thr, ROUNDS + 1)
            dve.tensor_scalar(above[:], sv[:], thr[:, 0:1], 0.0, ALU.is_gt, ALU.add, accum_out=ends[:, 0:1])
            dve.tensor_scalar(equal[:], sv[:], thr[:, 0:1], None, ALU.is_equal).then_inc(s_pick, 1)
            dve.wait_ge(s_pick, 1)
            dve.tensor_tensor_scan(scan[:], equal[:], equal[:], 0.0, ALU.add, ALU.max).then_inc(s_sel, 1)
            dve.wait_ge(s_tot, ROUNDS + 1)
            dve.tensor_copy(ends[:, 1:3], ps[:, 1, 0:2]).then_inc(s_pick, 1)
            dve.wait_ge(s_pick, 2)
            dve.tensor_tensor(need[:], ends[:, 1:2], ends[:, 2:3], ALU.add).then_inc(s_pick, 1)
            dve.wait_ge(s_pick, 3)
            dve.tensor_scalar(junk[:, 0, :], scan[:], need[:, 0:1], float(KSEL), ALU.add, ALU.is_le).then_inc(s_pick, 1)
            dve.wait_ge(s_pick, 4)
            dve.tensor_tensor(junk[:, 1, :], junk[:, 0, :], equal[:], ALU.mult).then_inc(s_pick, 1)
            dve.wait_ge(s_pick, 5)
            dve.tensor_tensor(chosen[:], junk[:, 1, :], above[:], ALU.add).then_inc(s_pick, 1)
            dve.wait_ge(s_pick, 6)
            dve.tensor_tensor_scan(place[:], chosen[:], chosen[:], 0.0, ALU.add, ALU.max).then_inc(s_sel, 1)
            dve.wait_ge(s_tot, ROUNDS + 2)
            dve.tensor_copy(ends[:, 3:4], ps[:, 1, 0:1]).then_inc(s_pick, 1)
            dve.wait_ge(s_pick, 7)
            dve.scalar_tensor_tensor(out=scan[:], in0=place[:], scalar=ends[:, 3:4], in1=chosen[:],
                                     op0=ALU.add, op1=ALU.mult).then_inc(s_pick, 1)
            dve.wait_ge(s_pickmm, 1)
            dve.tensor_scalar(slot_i[:], ps[:, 0, 0:CH], -1.0, None, ALU.add).then_inc(s_slot, 1)
            dve.wait_ge(s_slot, 1)
            dve.tensor_scalar(part_i[:], slot_i[:], KT.bit_length() - 1, None, ALU.arith_shift_right).then_inc(s_slot, 1)
            dve.tensor_scalar(four_i[:], slot_i[:], KT - 1, None, ALU.bitwise_and).then_inc(s_slot, 1)
            dve.wait_ge(s_slot, 3)
            dve.tensor_copy(part_f[:], part_i[:]).then_inc(s_slot, 1)
            dve.tensor_copy(four_f[:], four_i[:]).then_inc(s_slot, 1)
            dve.wait_ge(s_slot, 5)

            def spread(e):
                shape = [P, NT, KT]
                part = part_f[:].rearrange("p (s e) -> p s e", e=E)[:, :, bass.ds(e, 1)]
                four = four_f[:].rearrange("p (s e) -> p s e", e=E)[:, :, bass.ds(e, 1)]
                dve.tensor_tensor(eq4[:], four.to_broadcast(shape),
                                  cs[:, C_FOUR:C_FOUR + KT].unsqueeze(1).to_broadcast(shape), ALU.is_equal).then_inc(s_eq4, 1)
                dve.wait_ge(s_eq4, e + 1)
                dve.tensor_tensor(pay[:, :, 0, :], eq4[:], cs[:, C_TILE:C_TILE + NT].unsqueeze(2).to_broadcast(shape), ALU.mult)
                dve.tensor_scalar(pay[:, :, 1, :], eq4[:], cs[:, C_PART:C_PART + 1], None, ALU.mult)
                dve.tensor_tensor(hot, part.to_broadcast([P, NT, P]),
                                  cs[:, C_IOTA:C_IOTA + P].unsqueeze(1).to_broadcast([P, NT, P]), ALU.is_equal).then_inc(s_hot, 1)

            def numbers(e, k):
                dve.wait_ge(s_idmm, e + 1)
                dve.tensor_copy(idp[:], ps[:, 6, 0:2 * KT]).then_inc(s_idp, 1)
                dve.wait_ge(s_idp, e + 1)
                dve.scalar_tensor_tensor(out=idx[:, k, :], in0=idp[:, 0:KT], scalar=float(P), in1=idp[:, KT:2 * KT],
                                         op0=ALU.mult, op1=ALU.add).then_inc(s_idx, 1)

            def gates(e, k):
                dve.wait_ge(s_gat, 16 * KT * e + 16 * KT)
                dve.tensor_copy(gate[:, k, :].unsqueeze(2), xg[:, :, bass.ds(D + e, 1)]).then_inc(s_gate, 1)

            def expert(g, k, last):
                e = GS * g + k
                if not last:
                    numbers(e + 1, 1 - k)
                    if last is False:
                        spread(e + 2)
                    gates(e + 1, 1 - k)
                dve.wait_ge(s_ybfree, e + 1)
                dve.tensor_copy(idx_add[:], idx[:, k, :]).then_inc(s_idadd, 1)
                for j in range(KT):
                    dve.wait_ge(s_dmm, KT * e + (j + 1))
                    dve.tensor_scalar(yb[:, j, :], ps[:, 4 + j % 2, 0:D], gate[:, k, j:j + 1], None, ALU.mult).then_inc(s_y, 1)

            dve.sem_inc(s_y, 2)
            spread(0)
            numbers(0, 0)
            spread(1)
            gates(0, 0)
            with dve.Fori(0, G - 1) as g:
                for k in range(GS):
                    expert(g, k, False)
            expert(G - 1, 0, 0)
            expert(G - 1, 1, True)

            def last_norm(i, half):
                b = 2 * i + half
                dve.wait_ge(s_yin[half], 16 * i + 16)
                dve.wait_ge(s_fnm, 2 * b + 2)
                for t in range(TB):
                    dve.bn_stats(fst[:, t % 2, :], h_all[:, bass.ds(b * TB + t, 1), 0:D].rearrange("p a d -> p (a d)")).then_inc(s_fst, 1)
                    stand(dve, s_fst, TB * b + (t + 1))
                    dve.bn_aggr(fmv[:, half, t, :], fst[:, t % 2, :]).then_inc(s_fmv, 1)

            with dve.Fori(0, NB // 2) as i:
                for half in range(2):
                    last_norm(i, half)

        @block.scalar
        def _(act):
            def keys(i, j, kind):
                if not has(kind, j, 0):
                    return
                act.wait_ge(s_kx, 4 * i + (j + 3))
                if kind != "first" or j >= 2:
                    act.wait_ge(s_key, 4 * i + (j - 1))
                act.activation(kneg[:, j % 2, :], kx[:, j % 2, :], ACT.Relu, scale=-1.0).then_inc(s_kneg, 1)
                act.wait_ge(s_kneg, 4 * i + (j + 1))
                act.activation(kexp[:, j % 2, :], kneg[:, j % 2, :], ACT.Exp, scale=-1.0).then_inc(s_kexp, 1)

            pair_steps(act, keys)

            def queries(n, m):
                act.wait_ge(s_qmm, C * n + (m + 1))
                act.activation(qrel[:, m, :], ps[:, m, :], ACT.Relu, bias=bq_s[:, m:m + 1])
                act.activation(qexp[:, m, :], ps[:, m, :], ACT.Exp, bias=bq_s[:, m:m + 1]).then_inc(s_qread, 1)

            def regroup(row, t):
                act.dma_start(att[:, t % TB:t % TB + 1, :], heads[:, bass.ds(row, 1), :]).then_inc(s_attin[t % 2], 16)

            def tokens(n, t, kind):
                tile = TB * (n - HALF) + t
                if prefetches(kind) and t < C:
                    act.wait_ge(s_q, C * n + (t + 1))
                    queries(n + 1, t)
                if kind == "begin" and t == 0:
                    act.wait_ge(s_att, PER + 2)
                    for row in range(2):
                        regroup(row, row)
                if has_row(kind, t, 0):
                    act.wait_ge(s_attmm, tile + 1)
                    act.copy(att_t[:, t].rearrange("p c k -> p (c k)"), ps[:, 4, 0:D]).then_inc(s_attt, 1)
                if has_row(kind, t, 3):
                    act.wait_ge(s_x1mm, tile - 2)
                    act.copy(x1t[:, (t - 3) % TB].rearrange("p c k -> p (c k)"), ps[:, 7, 0:D]).then_inc(s_x1t, 1)
                if has_row(kind, t, 0) and not (kind == "last" and t >= TB - 2):
                    if kind == "attended" and t == TB - 2:
                        act.wait_ge(s_att, NT + 2)
                    regroup(tile + 2, t + 2)

            act.wait_ge(s_wts, 16 * 9)
            for m in range(C):
                queries(0, m)
            tile_steps(act, tokens)

            act.wait_ge(s_soft, 2)
            act.activation(lg[:], prob[:], ACT.Exp).then_inc(s_exp, 1)

            def turn(e):
                act.wait_ge(s_xtmm, e + 1)
                for c in range(C):
                    act.copy(xgt[:, c, :], ps[:, 2 + c, :]).then_inc(s_xt, 1)

            def expert(g, k, last):
                e = GS * g + k
                for f in range(FT):
                    width = P if f < FT - 1 else FR
                    stand(act, s_umm, FT * e + (f + 1))
                    act.activation(mid[0:width, f, :], ps[0:width, f % 2, :], ACT.Silu,
                                   bias=bup_s[0:width, bass.ds(g, 1), f:f + 1].rearrange("p a f -> p (a f)")).then_inc(s_mid, 1)
                if not last:
                    turn(e + 1)

            act.sem_inc(s_mid, 2)
            turn(0)
            with act.Fori(0, G - 1) as g:
                for k in range(GS):
                    expert(g, k, False)
            expert(G - 1, 0, False)
            expert(G - 1, 1, True)

            def last_norm(i, half):
                b = 2 * i + half
                stand(act, s_fnm, 2 * b + 6)
                for t in range(TB):
                    row = h_all[:, bass.ds(b * TB + t, 1), 0:D].rearrange("p a d -> p (a d)")
                    act.activation(row, row, ACT.Identity, bias=fnm[:, half, t:t + 1], scale=frs[:, half, t:t + 1]).then_inc(s_fin, 1)

            act.sem_inc(s_fin, 2 * TB)
            with act.Fori(0, NB // 2) as i:
                for half in range(2):
                    last_norm(i, half)

        @block.gpsimd
        def _(pool):
            def tokens(n, t, kind):
                tile = TB * (n - HALF) + t
                if has_row(kind, t, 2):
                    u = (t - 2) % TB
                    pool.wait_ge(s_mv2, tile - 1)
                    pool.tensor_tensor(ve2[:, u:u + 1], mv2[:, u, 1:2], cs[:, C_EPS:C_EPS + 1], ALU.add).then_inc(s_ve2, 1)
                    pool.wait_ge(s_ve2, tile - 1)
                    pool.tensor_tensor(rstd2[:, u:u + 1], ve2[:, u:u + 1], cs[:, C_HALF:C_HALF + 1], ALU.pow).then_inc(s_rs2, 1)
                if has_row(kind, t, 1):
                    u = (t - 1) % TB
                    row = h_all[:, bass.ds(tile - 1, 1), 0:D].rearrange("p a d -> p (a d)")
                    pool.tensor_tensor(xx[:, u % 2, :], row, row, ALU.add).then_inc(s_xx, 1)
                    pool.wait_ge(s_xx, tile)
                    pool.tensor_tensor(xb[:, u, :], xx[:, u % 2, :], rw[:, R_BETA:R_BETA + D], ALU.add).then_inc(s_xb, 1)
                    pool.wait_ge(s_mv, tile)
                    pool.tensor_tensor(ve[:, u:u + 1], mv[:, u, 1:2], cs[:, C_EPS:C_EPS + 1], ALU.add).then_inc(s_ve, 1)
                    pool.wait_ge(s_ve, tile)
                    pool.tensor_tensor(rstd[:, u:u + 1], ve[:, u:u + 1], cs[:, C_HALF:C_HALF + 1], ALU.pow).then_inc(s_rs, 1)

            pool.wait_ge(s_keyw, 32)
            pool.wait_ge(s_wts, 16 * 9)
            for half in range(2):
                pool.wait_ge(s_h[half], 16 * (NB // 2))
            tile_steps(pool, tokens)

            pool.wait_ge(s_x1out, 32 * NT)
            pool.wait_ge(s_probout, 16)

            def gather(e, k, slot_used):
                if slot_used:
                    pool.wait_ge(s_xtmm, e)
                    pool.wait_ge(s_gate, e)
                stand(pool, s_idx, e + 1)
                for j in range(KT):
                    pool.indirect_dma_start(out=xg[:, j, :], out_offset=None, in_=table[:, :],
                                            in_offset=bass.IndirectOffsetOnAxis(ap=idx[:, k, j:j + 1], axis=0)).then_inc(s_gat, 16)

            def add_rows(e):
                pool.wait_ge(s_y, KT * e + (KT + 2))
                stand(pool, s_idadd, e + 1)
                for j in range(KT):
                    pool.indirect_dma_start(out=ysum[:, :], out_offset=bass.IndirectOffsetOnAxis(ap=idx_add[:, j:j + 1], axis=0),
                                            in_=yb[:, j, :], in_offset=None, compute_op=ALU.add).then_inc(s_add, 16)
                pool.wait_ge(s_add, 16 * KT * e + 16 * KT)
                pool.sem_inc(s_ybfree, 1)

            pool.sem_inc(s_ybfree, 1)
            gather(0, 0, False)
            with pool.Fori(0, G - 1) as g:
                for k in range(GS):
                    gather(GS * g + (k + 1), 1 - k, True)
                    add_rows(GS * g + k)
            gather(E - 1, 1, True)
            add_rows(E - 2)
            add_rows(E - 1)

            def last_norm(i, half):
                b = 2 * i + half
                pool.wait_ge(s_fmv, TB * b + TB)
                pool.wait_ge(s_fin, TB * b + TB)
                pool.tensor_tensor(fve[:, half, :], fmv[:, half, :, 1], cs[:, C_EPS:C_EPS + TB], ALU.add).then_inc(s_fve, 1)
                pool.wait_ge(s_fve, b + 1)
                pool.tensor_tensor(frs[:, half, :], fve[:, half, :], cs[:, C_HALF:C_HALF + TB], ALU.pow).then_inc(s_frs, 1)
                pool.wait_ge(s_frs, b + 1)
                pool.tensor_tensor(fnm[:, half, :], fmv[:, half, :, 0], frs[:, half, :], ALU.mult).then_inc(s_fnm, 1)
                pool.wait_ge(s_fnm, 2 * b + 5)
                pool.tensor_tensor(fnm[:, half, :], fnm[:, half, :], cs[:, C_NEG:C_NEG + TB], ALU.mult).then_inc(s_fnm, 1)

            pool.sem_inc(s_fnm, 4)
            with pool.Fori(0, NB // 2) as i:
                for half in range(2):
                    last_norm(i, half)


def kernel(L0_attn_H, L0_attn_W_qkv, L0_attn_b_qkv, L0_attn_W_proj, L0_attn_b_proj, L0_attn_gamma, L0_attn_beta,
           L0_ffn_Wr, L0_ffn_br, L0_ffn_W_up, L0_ffn_b_up, L0_ffn_W_down, L0_ffn_b_down):
    import concourse.bacc as bacc
    from concourse.bass_utils import run_bass_kernel_spmd

    x = np.asarray(L0_attn_H)[0]
    bqkv = np.asarray(L0_attn_b_qkv)
    rows = np.concatenate([bqkv[D:2 * D], L0_attn_b_proj, L0_attn_gamma, L0_attn_beta, L0_ffn_br])
    bup = np.zeros((G, FT * P), np.float32)
    bup[:, :F] = L0_ffn_b_up
    cst, steps = constants()
    xs = x.reshape(PER, 2, P, D).transpose(1, 0, 2, 3).reshape(N, D)
    xq = x.reshape(2, P, PER, D).transpose(0, 2, 1, 3).reshape(N, D)
    ins = {
        "x": xs,
        "xt": xs.T,
        "xtq": xq.T,
        "wqkv": np.asarray(L0_attn_W_qkv).T,
        "bq": bqkv[:D].reshape(C, P).T,
        "bv": bqkv[2 * D:].reshape(1, D),
        "wp": np.asarray(L0_attn_W_proj).T,
        "rows": np.broadcast_to(rows, (P, R_ALL)),
        "wr": np.asarray(L0_ffn_Wr),
        "wup": np.asarray(L0_ffn_W_up),
        "bup": bup.reshape(G, FT, P).transpose(2, 0, 1),
        "wdn": np.concatenate([L0_ffn_W_down, np.asarray(L0_ffn_b_down)[:, None, :]], axis=1),
        "cst": cst,
        "steps": steps,
    }
    nc = bacc.Bacc("TRN2", target_bir_lowering=False, num_devices=1)
    arrays, args = {}, []
    for name, a in ins.items():
        a = np.ascontiguousarray(a)
        arrays[name] = a
        args.append(nc.dram_tensor(name, a.shape, mybir.dt.from_np(a.dtype), kind="ExternalInput").ap())
    args.append(nc.dram_tensor("out", (N, D), F32, kind="ExternalOutput").ap())
    build(nc, *args)
    r = run_bass_kernel_spmd(nc, [arrays], core_ids=[0])
    return r.results[0]["out"].reshape(2, PER, P, D).transpose(1, 0, 2, 3).reshape(1, N, D)
```

```python
from contextlib import ExitStack

import numpy as np

import concourse.bass as bass
from concourse import mybir

P = 128
ALU = mybir.AluOpType
ACT = mybir.ActivationFunctionType
AX = mybir.AxisListType
F32 = mybir.dt.float32
BF16 = mybir.dt.bfloat16
I32 = mybir.dt.int32

N = 4096
D = 256
C = D // P
HEADS = 16
HD = D // HEADS
HH = HEADS // C
TB = 4
BLK = TB * P
NT = N // P
NB = NT // TB
E = 8
GS = 2
G = E // GS
F = int(D * 4 * (2.0 / 3.0))
FT = -(-F // P)
FR = F - (FT - 1) * P
KSEL = N // E
KT = KSEL // P
EPS = 1e-5
ROW = D + E
HC = D + 2
CH = 2 * P
NCH = N // CH
BITS = 30
RB = 2
ROUNDS = BITS // RB
LATE = E - GS
NORMS = NT + GS * KT
CAND = (1 << RB) - 1

C_ID, C_HEAD, C_SAME, C_BEFORE, C_IOTA = (P * i for i in range(5))
C_HEAD8 = 5 * P
C_FOUR = C_HEAD8 + HH
C_TILE = C_FOUR + KT
C_PART = C_TILE + NT
C_HALF = C_PART + 1
C_EPS = C_HALF + 2 * TB
C_NEG = C_EPS + 2 * TB
C_PICK = C_NEG + 2 * TB
C_ALL = C_PICK + P
R_BK, R_BP, R_GAMMA, R_BETA = (D * i for i in range(4))
R_BR = 4 * D
R_ALL = R_BR + E
PER = N // 2 // P
PARTS = 3
HALF = PER // TB


def constants():
    p = np.arange(P)
    c = np.zeros((P, C_ALL), np.float32)
    c[:, C_ID:C_ID + P] = np.eye(P)
    c[:, C_HEAD:C_HEAD + P] = p[:, None] // HD == p // HD
    c[:, C_SAME:C_SAME + P] = p[:, None] % E == p % E
    c[:, C_BEFORE:C_BEFORE + P] = (p[:, None] % E == p % E) & (p[:, None] < p)
    c[:, C_IOTA:C_IOTA + P] = p
    c[:, C_HEAD8:C_HEAD8 + HH] = p[:, None] // HD == np.arange(HH)
    c[:, C_FOUR:C_FOUR + KT] = np.arange(KT)
    c[:, C_TILE:C_TILE + NT] = np.arange(NT)
    c[:, C_PART] = p
    c[:, C_HALF:C_HALF + 2 * TB] = -0.5
    c[:, C_EPS:C_EPS + 2 * TB] = EPS
    c[:, C_NEG:C_NEG + 2 * TB] = -1.0
    c[:, C_PICK:C_PICK + P] = ((p % 32 == 0) & (p // 32 < PARTS))[:, None]
    steps = [j << (BITS - RB * (r + 1)) for r in range(ROUNDS) for j in range(1, CAND + 1)]
    return c, np.tile(np.array(steps, np.int32), (P, 1))


def build(nc, x, xt, xtq, wqkv, bq, bv, wp, rows, wr, wup, bup, wdn, cst, steps, out):
    with ExitStack() as ctx:
        def sb(name, shape, dt=F32):
            return ctx.enter_context(nc.sbuf_tensor(name, shape, dt))

        def sem(name):
            return ctx.enter_context(nc.semaphore(name))

        table = nc.dram_tensor("table", [N, ROW], F32, kind="Internal").ap()
        ysum = nc.dram_tensor("ysum", [N, D], F32, kind="Internal").ap()

        ps = ctx.enter_context(nc.psum_tensor("ps", [P, 8, 512], F32))

        cs = sb("cs", [P, C_ALL])
        stp = sb("stp", [P, ROUNDS * CAND], I32)
        rw = sb("rw", [P, R_ALL])
        wqkv_s = sb("wqkv_s", [P, C, 3 * D])
        wp_s = sb("wp_s", [P, C, D])
        wr_s = sb("wr_s", [P, C, E])
        bq_s = sb("bq_s", [P, C])
        bv_s = sb("bv_s", [1, D])
        bup_s = sb("bup_s", [P, G, FT])
        h_all = sb("h_all", [P, NT, HC])
        ht_all = sb("ht_all", [P, C, N])
        heads = sb("heads", [P, NT, D])
        early = heads[:].rearrange("p t d -> p (t d)")
        ht_ring = early[:, 0:2 * C * BLK].rearrange("p (a c n) -> p a c n", a=2, c=C)
        kx, kneg, kexp = (early[:, at * D:(at + 4) * D].rearrange("p (a d) -> p a d", a=2) for at in (8, 12, 16))
        key = early[:, 20 * D:28 * D].rearrange("p (a u d) -> p a u d", a=4, u=2)
        kh = sb("kh", [P, C, HC])
        kht = sb("kht", [P, C, D])
        k1row = sb("k1row", [1, D])
        kvk = sb("kvk", [P, C, P + HH])
        qrel = sb("qrel", [P, C, BLK])
        qexp = sb("qexp", [P, C, BLK])
        qt = sb("qt", [P, C, BLK])
        den = sb("den", [P, TB, HEADS])
        rden = sb("rden", [P, TB, HEADS])
        att = sb("att", [P, TB, D])
        turned = sb("turned", [P, TB, 2 * C, P])
        zg = sb("zg", [P, TB, D])
        st = sb("st", [P, 2, 6])
        mv = sb("mv", [P, TB, 2])
        mv2 = sb("mv2", [P, TB, 2])
        ve = sb("ve", [P, TB])
        ve2 = sb("ve2", [P, TB])
        nm = sb("nm", [P, TB])
        rstd = sb("rstd", [P, TB])
        rstd2 = sb("rstd2", [P, TB])
        shift2 = sb("shift2", [P, TB])
        us = sb("us", [P, TB, D])
        x1 = sb("x1", [P, TB, D])
        bp_left = sb("bp_left", [P, D])
        bp_parts = sb("bp_parts", [PARTS * 32, D], BF16)
        pick_parts = sb("pick_parts", [PARTS * 32, P], BF16)
        lg = sb("lg", [P, NT, E])
        mx = sb("mx", [P, NT])
        sm = sb("sm", [P, NT])
        prob = sb("prob", [P, NT, E])
        sv = sb("sv", [P, CH])
        cand = sb("cand", [P, CAND], I32)
        thr = sb("thr", [P, 1 + CAND])
        cnt = sb("cnt", [P, CAND], BF16)
        same = sb("same", [P, P], BF16)
        junk = sb("junk", [P, CAND, CH])
        chosen = sb("chosen", [P, CH])
        place = sb("place", [P, CH])
        above = sb("above", [P, CH])
        equal = sb("equal", [P, CH])
        scan = sb("scan", [P, CH])
        ends = sb("ends", [P, 4])
        need = sb("need", [P, 1])
        slot_i = sb("slot_i", [P, CH], I32)
        part_i = sb("part_i", [P, CH], I32)
        part_f = sb("part_f", [P, CH])
        four_i = sb("four_i", [P, CH], I32)
        four_f = sb("four_f", [P, CH])
        dead = ht_all[:].rearrange("p c n -> p (c n)")
        mid = dead[:, 0:FT * KSEL].rearrange("p (f k) -> p f k", f=FT)
        hot = dead[:, FT * KSEL:FT * KSEL + NT * P // 2].bitcast(BF16).rearrange("p (s k) -> p s k", s=NT)
        spare = sb("spare", [P, 1])
        eq4 = sb("eq4", [P, NT, KT])
        pay = sb("pay", [P, NT, 2, KT], BF16)
        idp = sb("idp", [P, 2 * KT])
        idx = sb("idx", [P, 2, KT], I32)
        idx_add = sb("idx_add", [P, KT], I32)
        gate = sb("gate", [P, 2, KT])
        wup_s = sb("wup_s", [P, C, F])
        wdn_s = sb("wdn_s", [P, FT, D])
        xg = sb("xg", [P, KT, ROW])
        xgt = sb("xgt", [P, C, KSEL])
        yb = sb("yb", [P, KT, D])
        y_late = early[:, 0:KT * D].rearrange("p (j d) -> p j d", j=KT)
        o_late = early[:, KT * D:3 * KT * D].rearrange("p (k j d) -> p k j d", k=GS, j=KT)
        stats = early[:, 3 * KT * D:4 * KT * D]
        fst = stats[:, 0:TB * 6].rearrange("p (t s) -> p t s", t=TB)
        fmv = stats[:, 32:32 + 2 * NORMS].rearrange("p (t s) -> p t s", s=2)
        fve, frs, fmr, fnm = (stats[:, at:at + NORMS] for at in range(32 + 2 * NORMS, 32 + 6 * NORMS, NORMS))

        s_stood = sem("s_stood")
        s_keyw = sem("s_keyw")
        s_rows = sem("s_rows")
        s_wts = sem("s_wts")
        s_ring = [sem(f"s_ring{i}") for i in range(2)]
        s_h = [sem(f"s_h{i}") for i in range(2)]
        s_ht = sem("s_ht")
        s_x2b = sem("s_x2b")
        s_ones = sem("s_ones")
        s_kmm = sem("s_kmm")
        s_kx = sem("s_kx")
        s_kneg = sem("s_kneg")
        s_kexp = sem("s_kexp")
        s_key = sem("s_key")
        s_khmm = sem("s_khmm")
        s_kh = sem("s_kh")
        s_khtmm = sem("s_khtmm")
        s_kht = sem("s_kht")
        s_kvmm = sem("s_kvmm")
        s_kv = sem("s_kv")
        s_qmm = sem("s_qmm")
        s_qact = sem("s_qact")
        s_qread = sem("s_qread")
        s_q = sem("s_q")
        s_amm = sem("s_amm")
        s_den = sem("s_den")
        s_att = sem("s_att")
        s_attin = [sem(f"s_attin{i}") for i in range(TB)]
        s_parts = sem("s_parts")
        s_turnmm = sem("s_turnmm")
        s_turned = sem("s_turned")
        s_zmm = sem("s_zmm")
        s_st = sem("s_st")
        s_st2 = sem("s_st2")
        s_mv = sem("s_mv")
        s_zg = sem("s_zg")
        s_ve = sem("s_ve")
        s_rs = sem("s_rs")
        s_us = sem("s_us")
        s_mv2 = sem("s_mv2")
        s_ve2 = sem("s_ve2")
        s_nm = sem("s_nm")
        s_rs2 = sem("s_rs2")
        s_shift2 = sem("s_shift2")
        s_x1 = sem("s_x1")
        s_x1out = [sem(f"s_x1out{i}") for i in range(TB)]
        s_lmm = sem("s_lmm")
        s_lg = sem("s_lg")
        s_soft = sem("s_soft")
        s_exp = sem("s_exp")
        s_prob = sem("s_prob")
        s_probout = sem("s_probout")
        s_svmm = sem("s_svmm")
        s_thr = sem("s_thr")
        s_kept = sem("s_kept")
        s_cand = sem("s_cand")
        s_cnt = sem("s_cnt")
        s_tot = sem("s_tot")
        s_sel = sem("s_sel")
        s_pick = sem("s_pick")
        s_pickmm = sem("s_pickmm")
        s_slot = sem("s_slot")
        s_spare = sem("s_spare")
        s_wup = sem("s_wup")
        s_wdn = sem("s_wdn")
        s_eq4 = sem("s_eq4")
        s_hot = sem("s_hot")
        s_idmm = sem("s_idmm")
        s_idp = sem("s_idp")
        s_idx = sem("s_idx")
        s_gat = sem("s_gat")
        s_gate = sem("s_gate")
        s_xtmm = sem("s_xtmm")
        s_xt = sem("s_xt")
        s_umm = sem("s_umm")
        s_mid = sem("s_mid")
        s_midone = sem("s_midone")
        s_dmm = sem("s_dmm")
        s_y = sem("s_y")
        s_idadd = sem("s_idadd")
        s_ybfree = sem("s_ybfree")
        s_add = sem("s_add")
        s_yin = [sem(f"s_yin{i}") for i in range(NB)]
        s_ylate = sem("s_ylate")
        s_into = sem("s_into")
        s_fst = sem("s_fst")
        s_fmv = sem("s_fmv")
        s_fve = sem("s_fve")
        s_frs = sem("s_frs")
        s_fmr = sem("s_fmr")
        s_fnm = sem("s_fnm")
        s_fin = sem("s_fin")
        s_fin_last = sem("s_fin_last")
        s_out = sem("s_out")
        s_late = sem("s_late")

        ident = cs[:, C_ID:C_ID + P]
        table_t = table.rearrange("(s p) c -> p s c", p=P)
        ysum_t = ysum.rearrange("(s p) c -> p s c", p=P)
        out_t = out.rearrange("(s p) c -> p s c", p=P)
        x_t = x.rearrange("(s p) c -> p s c", p=P)
        xt_t = xt.rearrange("(c p) n -> p c n", p=P)
        xtq_t = xtq.rearrange("(c p) n -> p c n", p=P)

        block = ctx.enter_context(nc.Block())

        def pair_steps(eng, step):
            for j in range(4):
                step(0, j, "first")
            with eng.Fori(1, NB // 2 - 1) as i:
                for j in range(4):
                    step(i, j, "loop")
            for j in range(4):
                step(NB // 2 - 1, j, "last")
            for j in range(2):
                step(NB // 2, j, "drain")

        def tile_steps(eng, step):
            for kind, begin, end in (("attend", 0, HALF), ("begin", HALF, HALF + 1), ("second", HALF + 1, HALF + 2), ("both", HALF + 2, NB - 1),
                                     ("attended", NB - 1, NB), ("rows", NB, NB + HALF - 1),
                                     ("last", NB + HALF - 1, NB + HALF), ("drain", NB + HALF, NB + HALF + 1), ("end", NB + HALF + 1, NB + HALF + 2)):
                if end - begin == 1:
                    for t in range(TB):
                        step(begin, t, kind)
                else:
                    with eng.Fori(begin, end) as n:
                        for t in range(TB):
                            step(n, t, kind)

        def attends(kind):
            return kind in ("attend", "begin", "second", "both", "attended")

        def prefetches(kind):
            return kind in ("attend", "begin", "second", "both")

        def has_row(kind, t, lag):
            return {"attend": False, "begin": t >= lag, "second": TB + t >= lag,
                    "drain": t < lag, "end": TB + t < lag}.get(kind, True)

        def stand(eng, semaphore, value):
            eng.wait_ge(semaphore, value)
            eng.sem_inc(s_stood, 1)

        def has(kind, t, lag):
            return {"first": t >= lag, "drain": t < lag}.get(kind, True)

        @block.sync
        def _(sp):
            sp.dma_start(wqkv_s[:, :, D:2 * D], wqkv.rearrange("(c p) e -> p c e", p=P)[:, :, D:2 * D]).then_inc(s_keyw, 16)
            def load_block(i, half):
                b = 2 * i + half
                cols = bass.ds(b * BLK, BLK)
                sp.dma_start(ht_ring[:, half], xt_t[:, :, cols]).then_inc(s_ring[half], 16)
                sp.dma_start(h_all[:, bass.ds(b * TB, TB), 0:D], x_t[:, bass.ds(b * TB, TB), :]).then_inc(s_h[half], 16)

            sp.dma_start(ht_ring[:, 0], xt_t[:, :, 0:BLK]).then_inc(s_ring[0], 16)
            sp.dma_start(rw[:], rows).then_inc(s_rows, 16)
            sp.dma_start(h_all[:, 0:TB, 0:D], x_t[:, 0:TB, :]).then_inc(s_h[0], 16)
            load_block(0, 1)
            sp.dma_start(cs[:], cst).then_inc(s_wts, 16)
            sp.dma_start(stp[:], steps).then_inc(s_wts, 16)
            for half in (0, 1):
                sp.dma_start(wqkv_s[:, :, 2 * D * half:2 * D * half + D],
                             wqkv.rearrange("(c p) e -> p c e", p=P)[:, :, 2 * D * half:2 * D * half + D]).then_inc(s_wts, 16)
            sp.dma_start(wp_s[:], wp.rearrange("(c p) e -> p c e", p=P)).then_inc(s_wts, 16)
            sp.dma_start(wr_s[:], wr.rearrange("(c p) e -> p c e", p=P)).then_inc(s_wts, 16)
            sp.dma_start(bq_s[:], bq).then_inc(s_wts, 16)
            sp.dma_start(bv_s[:], bv).then_inc(s_wts, 16)
            sp.dma_start(bup_s[:], bup).then_inc(s_wts, 16)
            def load_queries(b):
                cols = bass.ds(b * BLK, BLK)
                sp.dma_start(ht_all[:, :, cols], xtq_t[:, :, cols]).then_inc(s_ht, 16)

            with sp.Fori(1, NB // 2) as i:
                for half in range(2):
                    stand(sp, s_kmm, 4 * i + (2 * half - 2))
                    stand(sp, s_h[half], 16 * i)
                    load_block(i, half)
            load_queries(0)
            with sp.Fori(1, NB) as b:
                stand(sp, s_ht, 16 * b)
                load_queries(b)

            def load_up(g):
                sp.dma_start(wup_s[:], wup[bass.ds(g, 1)].rearrange("g (c p) f -> p (g c) f", p=P)).then_inc(s_wup, 16)

            def load_down(e):
                full = (FT - 1) * P
                sp.dma_start(wdn_s[:, 0:FT - 1, :],
                             wdn[bass.ds(e, 1), 0:full, :].rearrange("g (f p) d -> p (g f) d", p=P)).then_inc(s_wdn, 16)
                sp.dma_start(wdn_s[0:FR + 1, FT - 1:FT, :],
                             wdn[bass.ds(e, 1), full:F + 1, :].rearrange("g p d -> p g d")).then_inc(s_wdn, 16)

            load_up(0)
            load_down(0)

            def store(m, u):
                stand(sp, s_x1, TB * m + (u + 1 + TB))
                tile = TB * m + u
                sp.dma_start(table_t[:, bass.ds(tile, 1), 0:D], x1[:, u:u + 1, :]).then_inc(s_x1out[u], 16)
                sp.dma_start(ysum_t[:, bass.ds(tile, 1), :], x1[:, u:u + 1, :]).then_inc(s_x1out[u], 16)

            def regroup(row, t):
                sp.dma_start(att[:, t % TB:t % TB + 1, :], heads[:, bass.ds(row, 1), :]).then_inc(s_attin[t % TB], 16)

            def move(n, t, kind):
                row = TB * (n - HALF) + t
                if kind == "begin" and t == 0:
                    sp.wait_ge(s_att, PER + 2)
                    for first in range(3):
                        regroup(first, first)
                if has_row(kind, t, 4):
                    store(n - HALF - 1, t)
                if has_row(kind, t, 0) and not (kind == "last" and t > 0):
                    if kind == "attended" and t == TB - 3:
                        sp.wait_ge(s_att, NT + 2)
                    if kind != "begin" or t > 0:
                        stand(sp, s_turnmm, row)
                    regroup(row + 3, t + 3)

            for t in range(TB):
                sp.sem_inc(s_x1out[t], 32)
            tile_steps(sp, move)
            sp.wait_ge(s_prob, 1)
            with nc.allow_non_contiguous_dma(reason="eight probabilities a token"):
                sp.dma_start(table_t[:, :, D:ROW], prob[:]).then_inc(s_probout, 16)
            for e in range(1, GS):
                sp.wait_ge(s_dmm, KT * e)
                load_down(e)
            with sp.Fori(1, G - 1) as g:
                stand(sp, s_umm, GS * FT * g)
                load_up(g)
                for k in range(GS):
                    stand(sp, s_dmm, GS * KT * g + KT * k)
                    load_down(GS * g + k)
            sp.wait_ge(s_umm, FT * LATE)
            load_up(G - 1)
            sp.wait_ge(s_dmm, KT * LATE)
            load_down(LATE)
            sp.wait_ge(s_ybfree, LATE + 1)
            sp.wait_ge(s_gat, 16 * KT * E)
            sp.wait_ge(s_ylate, 16 * KT)
            for b in range(NB):
                tiles = slice(b * TB, (b + 1) * TB)
                sp.dma_start(h_all[:, tiles, 0:D], ysum_t[:, tiles, :]).then_inc(s_yin[b], 16)

            def store_block(b):
                tiles = slice(b * TB, (b + 1) * TB)
                sp.dma_start(out_t[:, tiles, :], h_all[:, tiles, 0:D]).then_inc(s_out, 16)

            for b in range(2):
                sp.wait_ge(s_fin, TB * (b + 1))
                store_block(b)
            sp.wait_ge(s_dmm, KT * (E - 1))
            load_down(E - 1)
            for b in range(2, NB // 2):
                sp.wait_ge(s_fin, TB * (b + 1))
                store_block(b)
            for b in range(NB // 2, NB - 2):
                sp.wait_ge(s_fin_last, TB * (b - NB // 2 + 1))
                store_block(b + 2)
                sp.wait_ge(s_fin, TB * (b + 1) + KT)
                store_block(b)
            sp.wait_ge(s_late, 16 * GS * KT)

        @block.tensor
        def _(pe):
            def keys(i, j, kind):
                bank = j % 2
                if has(kind, j, 0):
                    if j % 2 == 0:
                        pe.wait_ge(s_ring[j // 2], 16 * i + 16)
                    pe.wait_ge(s_kx, 4 * i + (j + 1))
                    for u in range(2):
                        for c in range(C):
                            at = (2 * (j % 2) + u) * P
                            mm = pe.matmul(ps[:, bank, u * D:(u + 1) * D], ht_ring[:, j // 2, c, at:at + P],
                                           wqkv_s[:, c, D:2 * D], start=(c == 0), stop=(c == C - 1))
                    mm.then_inc(s_kmm, 1)
                if has(kind, j, 2):
                    back = j - 2
                    pe.wait_ge(s_key, 4 * i + (back + 1))
                    if j % 2 == 0:
                        if j == 0:
                            pe.wait_ge(s_h[1], 16 * i)
                        else:
                            pe.wait_ge(s_h[0], 16 * i + 16)
                    for u in range(2):
                        for c in range(C):
                            begins = kind == "first" and back == 0 and u == 0
                            ends_ = kind == "drain" and j == 1 and u == 1
                            mm = pe.matmul(ps[:, 2 + c, 0:HC], key[:, back % 4, u, c * P:(c + 1) * P],
                                           h_all[:, bass.ds(i * 8 + (2 * back + u), 1), :].rearrange("p a h -> p (a h)"),
                                           start=begins, stop=ends_, skip_group_check=True)
                    mm.then_inc(s_khmm, 1)

            def queries(n, m):
                for c in range(C):
                    mm = pe.matmul(ps[:, m, :], wqkv_s[:, c, m * P:(m + 1) * P], ht_all[:, c, bass.ds(n * BLK, BLK)],
                                   start=(c == 0), stop=(c == C - 1))
                mm.then_inc(s_qmm, 1)

            pe.wait_ge(s_keyw, 16)
            pe.wait_ge(s_ones, 1)
            pair_steps(pe, keys)

            pe.wait_ge(s_wts, 16 * 9)
            pe.wait_ge(s_kx, NT // 2 + 2)
            pe.wait_ge(s_ht, 16)
            for m in range(C):
                queries(0, m)

            pe.wait_ge(s_kh, 2)
            for c in range(C):
                for h in range(C):
                    pe.transpose(ps[:, 4, h * D + c * P:h * D + (c + 1) * P], kh[:, c, h * P:(h + 1) * P], ident)
            for c in range(C):
                mm = pe.transpose(ps[0:1, 5, c * P:(c + 1) * P], kh[:, c, D:D + 1], ident)
            mm.then_inc(s_khtmm, 1)
            pe.wait_ge(s_kht, 2)
            for c in range(C):
                half = slice(c * P, (c + 1) * P)
                for h in range(C):
                    pe.matmul(ps[:, 6, half], kht[:, h, half], wqkv_s[:, h, 2 * D + c * P:2 * D + (c + 1) * P],
                              start=(h == 0), stop=False)
                mm = pe.matmul(ps[:, 6, half], k1row[:, half], bv_s[:, half], start=False, stop=True)
            mm.then_inc(s_kvmm, 1)

            def turn_tiles(n, t, kind):
                row = TB * (n - HALF) + t
                turns = 0
                if has_row(kind, t, 0) or has_row(kind, t, 5):
                    pe.wait_ge(s_turned, row + 1)
                if has_row(kind, t, 0):
                    pe.wait_ge(s_attin[t], 16 * (n - HALF) + 16)
                    for c in range(C):
                        mm = pe.transpose(ps[:, 4, c * P:(c + 1) * P], att[:, t, c * P:(c + 1) * P], ident)
                    turns = 1
                if has_row(kind, t, 5):
                    pe.wait_ge(s_x1, row - 4 + TB)
                    for c in range(C):
                        mm = pe.transpose(ps[:, 4, D + c * P:D + (c + 1) * P], x1[:, (t - 5) % TB, c * P:(c + 1) * P], ident)
                    turns = 1
                if turns:
                    mm.then_inc(s_turnmm, 1)

            def tokens(n, t, kind):
                row = TB * (n - HALF) + t
                if attends(kind):
                    if t % 2 == 0:
                        pe.wait_ge(s_q, 2 * n + (t // 2 + 1))
                    pe.wait_ge(s_att, TB * n + (t + 1))
                    for c in range(C):
                        mm = pe.matmul(ps[:, 2 + t % 2, c * (P + HH):(c + 1) * (P + HH)], qt[:, c, t * P:(t + 1) * P],
                                       kvk[:, c, :], start=True, stop=True)
                    mm.then_inc(s_amm, 1)
                if not (kind == "begin" and t == 0):
                    turn_tiles(n, t, kind)
                if has_row(kind, t, 6):
                    pe.wait_ge(s_turned, row + 1)
                    for c in range(C):
                        mm = pe.matmul(ps[:, 7, bass.ds((row - 6) * E, E)], turned[:, (t - 1) % TB, C + c, :], wr_s[:, c, :],
                                       start=(c == 0), stop=(c == C - 1))
                    mm.then_inc(s_lmm, 1)
                if has_row(kind, t, 1):
                    pe.wait_ge(s_turned, row + 1)
                    pe.wait_ge(s_zg, row)
                    bank = ps[:, 5 + (t - 1) % 2, 0:D]
                    pe.matmul(bank, pick_parts[:], bp_parts[:], start=True, stop=False)
                    for c in range(C):
                        mm = pe.matmul(bank, turned[:, (t - 1) % TB, c, :], wp_s[:, c, :], start=False, stop=(c == C - 1))
                    mm.then_inc(s_zmm, 1)
                if prefetches(kind) and t < C:
                    pe.wait_ge(s_qread, C * n + (t + 1))
                    if t == 0:
                        pe.wait_ge(s_ht, 16 * n + 32)
                    queries(n + 1, t)
                if kind == "begin" and t == 0:
                    turn_tiles(n, t, kind)

            pe.wait_ge(s_kv, 1)
            pe.wait_ge(s_parts, 8)
            tile_steps(pe, tokens)

            pe.wait_ge(s_prob, 1)
            for h in range(2):
                mm = pe.transpose(ps[:, 0, h * P:(h + 1) * P], prob[:, h * NCH:(h + 1) * NCH, :].rearrange("p i e -> p (i e)"), ident)
            mm.then_inc(s_svmm, 1)
            with pe.Fori(0, ROUNDS // 5) as turn:
                for k in range(5):
                    pe.wait_ge(s_cnt, 5 * turn + (k + 1))
                    pe.matmul(ps[:, 1, 0:CAND], same[:], cnt[:], start=True, stop=True).then_inc(s_tot, 1)
            pe.wait_ge(s_sel, 1)
            pe.matmul(ps[:, 1, 0:1], cs[:, C_SAME:C_SAME + P], ends[:, 0:1], start=True, stop=True)
            pe.matmul(ps[:, 1, 1:2], cs[:, C_BEFORE:C_BEFORE + P], scan[:, CH - 1:CH], start=True, stop=True).then_inc(s_tot, 1)
            pe.wait_ge(s_sel, 2)
            pe.matmul(ps[:, 1, 0:1], cs[:, C_BEFORE:C_BEFORE + P], place[:, CH - 1:CH], start=True, stop=True).then_inc(s_tot, 1)
            pe.wait_ge(s_pick, 8)
            for h in range(2):
                mm = pe.transpose(ps[:, 0, h * P:(h + 1) * P], scan[:, h * P:(h + 1) * P], ident)
            mm.then_inc(s_pickmm, 1)

            def lists(e):
                pe.wait_ge(s_hot, e + 1)
                for s in range(NT):
                    mm = pe.matmul(ps[:, 6, 0:2 * KT], hot[:, s, :], pay[:, s].rearrange("p w k -> p (w k)"),
                                   start=(s == 0), stop=(s == NT - 1))
                mm.then_inc(s_idmm, 1)

            def turn(e):
                pe.wait_ge(s_gat, 16 * KT * e + 16 * KT)
                for c in range(C):
                    for k in range(KT):
                        mm = pe.transpose(ps[:, 2 + c, k * P:(k + 1) * P], xg[:, k, c * P:(c + 1) * P], ident)
                mm.then_inc(s_xtmm, 1)

            def expert(g, k, last):
                e = GS * g + k
                if not last:
                    lists(e + 1)
                pe.wait_ge(s_xt, C * e + C)
                if k == 0:
                    pe.wait_ge(s_wup, 16 * g + 16)
                for f in range(FT):
                    width = P if f < FT - 1 else FR
                    pe.wait_ge(s_mid, e * FT + (f + 1))
                    for c in range(C):
                        mm = pe.matmul(ps[0:width, f % 2, :], wup_s[:, c, f * P:f * P + width], xgt[:, c, :],
                                       start=(c == 0), stop=(c == C - 1))
                    mm.then_inc(s_umm, 1)
                if not last:
                    turn(e + 1)
                pe.wait_ge(s_wdn, 32 * e + 32)
                for j in range(KT):
                    if last:
                        bank = (4, 5, 2, 3)[j]
                    else:
                        bank = 4 + j % 2
                    if not last or j < 2:
                        pe.wait_ge(s_y, e * KT + (j + 1))
                    for f in range(FT):
                        rows_ = P if f < FT - 1 else FR + 1
                        if j == 0:
                            pe.wait_ge(s_mid, e * FT + (f + 3))
                        mm = pe.matmul(ps[:, bank, 0:D], mid[0:rows_, f, j * P:(j + 1) * P], wdn_s[0:rows_, f, :],
                                       start=(f == 0), stop=(f == FT - 1))
                    mm.then_inc(s_dmm, 1)

            lists(0)
            turn(0)
            pe.wait_ge(s_midone, 1)
            with pe.Fori(0, G - 1) as g:
                for k in range(GS):
                    expert(g, k, False)
            for k in range(GS):
                expert(G - 1, k, k == GS - 1)

        @block.vector
        def _(dve):
            dve.memset(h_all[:, :, D:HC], 1.0).then_inc(s_ones, 1)
            dve.sem_inc(s_kx, 2)

            def keys(i, j, kind):
                if has(kind, j, 0):
                    dve.wait_ge(s_kmm, 4 * i + (j + 1))
                    if kind != "first" or j >= 2:
                        dve.wait_ge(s_key, 4 * i + (j - 1))
                    dve.tensor_tensor(kx[:, j % 2, :].rearrange("p (u d) -> p u d", u=2),
                                      ps[:, j % 2, :].rearrange("p (u d) -> p u d", u=2),
                                      rw[:, R_BK:R_BK + D].unsqueeze(1).to_broadcast([P, 2, D]), ALU.add).then_inc(s_kx, 1)
                if has(kind, j, 1):
                    dve.wait_ge(s_kexp, 4 * i + j)
                    b = (j - 1) % 2
                    dve.scalar_tensor_tensor(out=key[:, (j - 1) % 4].rearrange("p u d -> p (u d)"), in0=kx[:, b, :], scalar=0.0,
                                             in1=kexp[:, b, :], op0=ALU.max, op1=ALU.add).then_inc(s_key, 1)
                if kind in ("loop", "last"):
                    double(4 * i + (j - 4))

            def double(pair):
                dve.wait_ge(s_khmm, pair + 1)
                tiles = h_all[:, bass.ds(2 * pair, 2), 0:D]
                dve.scalar_tensor_tensor(out=tiles, in0=tiles, scalar=2.0,
                                         in1=rw[:, R_BETA:R_BETA + D].unsqueeze(1).to_broadcast([P, 2, D]),
                                         op0=ALU.mult, op1=ALU.add).then_inc(s_x2b, 1)

            dve.wait_ge(s_rows, 16)
            dve.tensor_copy(bp_parts[:], rw[0:PARTS * 32, R_BP:R_BP + D]).then_inc(s_parts, 1)
            done = 1
            for part in range(1, PARTS):
                at = slice(32 * part, 32 * part + 32)
                src = rw[at, R_BP:R_BP + D]
                for _ in range(part):
                    dve.wait_ge(s_parts, done)
                    dve.tensor_tensor(bp_left[at, :], src, bp_parts[at, :], ALU.subtract).then_inc(s_parts, 1)
                    dve.wait_ge(s_parts, done + 1)
                    dve.tensor_copy(bp_parts[at, :], bp_left[at, :]).then_inc(s_parts, 1)
                    src = bp_left[at, :]
                    done += 2
            pair_steps(dve, keys)

            def make_q(n, half):
                cols = slice(half * BLK // 2, (half + 1) * BLK // 2)
                if half == 0:
                    dve.wait_ge(s_qread, C * n + C)
                dve.scalar_tensor_tensor(out=qt[:, :, cols], in0=qexp[:, :, cols], scalar=1.0, in1=qrel[:, :, cols],
                                         op0=ALU.min, op1=ALU.add).then_inc(s_q, 1)

            dve.wait_ge(s_khmm, NT // 2)
            for c in range(C):
                dve.tensor_copy(kh[:, c, :], ps[:, 2 + c, 0:HC]).then_inc(s_kh, 1)
            dve.wait_ge(s_kh, 2)
            dve.wait_ge(s_wts, 16 * 9)
            for c in range(C):
                dve.tensor_scalar(kvk[:, c, P:P + HH], cs[:, C_HEAD8:C_HEAD8 + HH], kh[:, c, D:D + 1], None, ALU.mult)
            dve.wait_ge(s_khtmm, 1)
            dve.tensor_copy(kht[:].rearrange("p c d -> p (c d)"), ps[:, 4, :]).then_inc(s_kht, 1)
            dve.tensor_copy(k1row[:], ps[0:1, 5, 0:D]).then_inc(s_kht, 1)
            make_q(0, 0)
            make_q(0, 1)
            dve.wait_ge(s_kvmm, 1)
            dve.tensor_tensor(kvk[:, :, 0:P], ps[:, 6, 0:D].rearrange("p (c v) -> p c v", c=C),
                              cs[:, C_HEAD:C_HEAD + P].unsqueeze(1).to_broadcast([P, C, P]), ALU.mult).then_inc(s_kv, 1)
            dve.tensor_copy(pick_parts[:], cs[0:PARTS * 32, C_PICK:C_PICK + P]).then_inc(s_parts, 1)

            def tokens(n, t, kind):
                tile = TB * (n - HALF) + t
                if has_row(kind, t, 3):
                    u = (t - 3) % TB
                    dve.wait_ge(s_rs, tile - 2)
                    dve.wait_ge(s_zg, tile)
                    dve.wait_ge(s_x1, tile - 2)
                    dve.scalar_tensor_tensor(out=us[:, u, :], in0=zg[:, u, :], scalar=rstd[:, u:u + 1],
                                             in1=h_all[:, bass.ds(tile - 3, 1), 0:D].rearrange("p a d -> p (a d)"),
                                             op0=ALU.mult, op1=ALU.add).then_inc(s_us, 1)
                    dve.wait_ge(s_us, tile - 2)
                    dve.bn_stats(st[:, 1, :], us[:, u, :]).then_inc(s_st2, 1)
                if attends(kind):
                    dve.wait_ge(s_amm, TB * n + (t + 1))
                    bank = ps[:, 2 + t % 2, 0:C * (P + HH)].rearrange("p (c w) -> p c w", c=C)
                    dve.tensor_scalar(den[:, t].rearrange("p (c h) -> p c h", c=C), bank[:, :, P:P + HH], 1e-6, None,
                                      ALU.max).then_inc(s_den, 1)
                    dve.wait_ge(s_den, 2 * TB * n + (2 * t + 1))
                    dve.reciprocal(rden[:, t, :], den[:, t, :]).then_inc(s_den, 1)
                if has_row(kind, t, 1):
                    u = (t - 1) % TB
                    z_bank = ps[:, 5 + u % 2, 0:D]
                    dve.wait_ge(s_zmm, tile)
                    dve.bn_stats(st[:, 0, :], z_bank).then_inc(s_st, 1)
                if has_row(kind, t, 3):
                    stand(dve, s_st2, tile - 2)
                    dve.bn_aggr(mv2[:, (t - 3) % TB, :], st[:, 1, :]).then_inc(s_mv2, 1)
                if has_row(kind, t, 1):
                    stand(dve, s_st, tile)
                    dve.bn_aggr(mv[:, u, :], st[:, 0, :]).then_inc(s_mv, 1)
                if attends(kind):
                    w = 0 if kind == "attend" else 1
                    j = bass.ds(TB * (n - HALF * w) + t, 1)
                    dve.wait_ge(s_den, 2 * TB * n + (2 * t + 2))
                    dve.tensor_tensor(heads[:, PER * w:PER * (w + 1), :].rearrange("p (c h) (j d) -> p c h j d", c=C, j=PER)[:, :, :, j, :].rearrange("p c h j d -> p c h (j d)"),
                                      bank[:, :, 0:P].rearrange("p c (h d) -> p c h d", h=HH),
                                      rden[:, t, :].rearrange("p (c h) -> p c h", c=C).unsqueeze(3).to_broadcast([P, C, HH, HD]),
                                      ALU.mult).then_inc(s_att, 1)
                if prefetches(kind) and t >= TB // 2:
                    make_q(n + 1, t - TB // 2)
                if kind == "attend" and t == TB - 1:
                    double(n + (NT // 2 - HALF))
                if has_row(kind, t, 1):
                    dve.wait_ge(s_mv, tile)
                    dve.scalar_tensor_tensor(out=zg[:, u, :], in0=z_bank, scalar=mv[:, u, 0:1], in1=rw[:, R_GAMMA:R_GAMMA + D],
                                             op0=ALU.subtract, op1=ALU.mult).then_inc(s_zg, 1)

            dve.sem_inc(s_att, 2)
            dve.sem_inc(s_zg, 2)
            tile_steps(dve, tokens)

            wide = [P, NT, E]
            dve.wait_ge(s_lmm, NT)
            dve.tensor_tensor(lg[:], ps[:, 7, 0:NT * E].rearrange("p (s e) -> p s e", e=E),
                              rw[:, R_BR:R_BR + E].unsqueeze(1).to_broadcast([P, NT, E]), ALU.add).then_inc(s_lg, 1)
            dve.wait_ge(s_lg, 1)
            dve.tensor_reduce(mx[:], lg[:], AX.X, ALU.max).then_inc(s_soft, 1)
            dve.wait_ge(s_soft, 1)
            dve.tensor_tensor(prob[:], lg[:], mx[:].unsqueeze(2).to_broadcast(wide), ALU.subtract).then_inc(s_soft, 1)
            dve.wait_ge(s_exp, 1)
            dve.tensor_reduce(sm[:], lg[:], AX.X, ALU.add).then_inc(s_soft, 1)
            dve.wait_ge(s_soft, 3)
            dve.reciprocal(mx[:], sm[:]).then_inc(s_soft, 1)
            dve.wait_ge(s_soft, 4)
            dve.tensor_tensor(prob[:], lg[:], mx[:].unsqueeze(2).to_broadcast(wide), ALU.mult).then_inc(s_prob, 1)

            dve.memset(thr[:], 0.0).then_inc(s_thr, 1)
            dve.tensor_copy(same[:], cs[:, C_SAME:C_SAME + P])
            dve.memset(mid[0:64, FT - 1, :], 1.0).then_inc(s_midone, 1)
            dve.wait_ge(s_svmm, 1)
            dve.tensor_copy(sv[:], ps[:, 0, 0:CH]).then_inc(s_cand, 1)
            def search(r):
                dve.wait_ge(s_thr, r + 1)
                dve.tensor_tensor(cand[:], thr[:, 0:1].bitcast(I32).to_broadcast([P, CAND]), stp[:, bass.ds(r * CAND, CAND)],
                                  ALU.bitwise_or).then_inc(s_cand, 1)
                dve.wait_ge(s_cand, r + 2)
                for q in range(CAND):
                    last = dve.tensor_scalar(junk[:, q, :], sv[:], cand[:, q:q + 1].bitcast(F32), 0.0, ALU.is_ge, ALU.add,
                                             accum_out=cnt[:, q:q + 1])
                last.then_inc(s_cnt, 1)
                dve.wait_ge(s_tot, r + 1)
                dve.scalar_tensor_tensor(out=thr[:, 1:1 + CAND], in0=ps[:, 1, 0:CAND], scalar=KSEL - 0.5,
                                         in1=cand[:].bitcast(F32), op0=ALU.is_ge, op1=ALU.mult).then_inc(s_kept, 1)
                dve.wait_ge(s_kept, r + 1)
                dve.tensor_reduce(thr[:, 0:1], thr[:], AX.X, ALU.max).then_inc(s_thr, 1)

            with dve.Fori(0, ROUNDS // 5) as turn:
                for k in range(5):
                    search(5 * turn + k)
            dve.wait_ge(s_thr, ROUNDS + 1)
            dve.tensor_scalar(above[:], sv[:], thr[:, 0:1], 0.0, ALU.is_gt, ALU.add, accum_out=ends[:, 0:1])
            dve.tensor_scalar(equal[:], sv[:], thr[:, 0:1], None, ALU.is_equal).then_inc(s_pick, 1)
            dve.wait_ge(s_pick, 1)
            dve.tensor_tensor_scan(scan[:], equal[:], equal[:], 0.0, ALU.add, ALU.max).then_inc(s_sel, 1)
            dve.wait_ge(s_tot, ROUNDS + 1)
            dve.tensor_copy(ends[:, 1:3], ps[:, 1, 0:2]).then_inc(s_pick, 1)
            dve.wait_ge(s_pick, 2)
            dve.tensor_tensor(need[:], ends[:, 1:2], ends[:, 2:3], ALU.add).then_inc(s_pick, 1)
            dve.wait_ge(s_pick, 3)
            dve.tensor_scalar(junk[:, 0, :], scan[:], need[:, 0:1], float(KSEL), ALU.add, ALU.is_le).then_inc(s_pick, 1)
            dve.wait_ge(s_pick, 4)
            dve.tensor_tensor(junk[:, 1, :], junk[:, 0, :], equal[:], ALU.mult).then_inc(s_pick, 1)
            dve.wait_ge(s_pick, 5)
            dve.tensor_tensor(chosen[:], junk[:, 1, :], above[:], ALU.add).then_inc(s_pick, 1)
            dve.wait_ge(s_pick, 6)
            dve.tensor_tensor_scan(place[:], chosen[:], chosen[:], 0.0, ALU.add, ALU.max).then_inc(s_sel, 1)
            dve.wait_ge(s_tot, ROUNDS + 2)
            dve.tensor_copy(ends[:, 3:4], ps[:, 1, 0:1]).then_inc(s_pick, 1)
            dve.wait_ge(s_pick, 7)
            dve.scalar_tensor_tensor(out=scan[:], in0=place[:], scalar=ends[:, 3:4], in1=chosen[:],
                                     op0=ALU.add, op1=ALU.mult).then_inc(s_pick, 1)
            dve.wait_ge(s_pickmm, 1)
            dve.tensor_scalar(slot_i[:], ps[:, 0, 0:CH], -1.0, None, ALU.add).then_inc(s_slot, 1)
            dve.wait_ge(s_slot, 1)
            dve.tensor_scalar(part_i[:], slot_i[:], KT.bit_length() - 1, None, ALU.arith_shift_right).then_inc(s_slot, 1)
            dve.tensor_scalar(four_i[:], slot_i[:], KT - 1, None, ALU.bitwise_and).then_inc(s_slot, 1)
            dve.wait_ge(s_slot, 3)
            dve.tensor_copy(part_f[:], part_i[:]).then_inc(s_slot, 1)
            dve.tensor_copy(four_f[:], four_i[:]).then_inc(s_slot, 1)
            dve.wait_ge(s_slot, 5)

            def spread(e):
                shape = [P, NT, KT]
                part = part_f[:].rearrange("p (s e) -> p s e", e=E)[:, :, bass.ds(e, 1)]
                four = four_f[:].rearrange("p (s e) -> p s e", e=E)[:, :, bass.ds(e, 1)]
                dve.tensor_tensor(eq4[:], four.to_broadcast(shape),
                                  cs[:, C_FOUR:C_FOUR + KT].unsqueeze(1).to_broadcast(shape), ALU.is_equal).then_inc(s_eq4, 1)
                dve.wait_ge(s_eq4, e + 1)
                dve.tensor_tensor(pay[:, :, 0, :], eq4[:], cs[:, C_TILE:C_TILE + NT].unsqueeze(2).to_broadcast(shape), ALU.mult)
                dve.tensor_scalar(pay[:, :, 1, :], eq4[:], cs[:, C_PART:C_PART + 1], None, ALU.mult)
                dve.tensor_tensor(hot, part.to_broadcast([P, NT, P]),
                                  cs[:, C_IOTA:C_IOTA + P].unsqueeze(1).to_broadcast([P, NT, P]), ALU.is_equal).then_inc(s_hot, 1)

            def numbers(e, k):
                dve.wait_ge(s_idmm, e + 1)
                dve.tensor_copy(idp[:], ps[:, 6, 0:2 * KT]).then_inc(s_idp, 1)
                dve.wait_ge(s_idp, e + 1)
                dve.scalar_tensor_tensor(out=idx[:, k, :], in0=idp[:, 0:KT], scalar=float(P), in1=idp[:, KT:2 * KT],
                                         op0=ALU.mult, op1=ALU.add).then_inc(s_idx, 1)

            def gates(e, k):
                dve.wait_ge(s_gat, 16 * KT * e + 16 * KT)
                dve.tensor_copy(gate[:, k, :].unsqueeze(2), xg[:, :, bass.ds(D + e, 1)]).then_inc(s_gate, 1)

            def expert(g, k):
                e = GS * g + k
                numbers(e + 1, 1 - k)
                spread(e + 2)
                gates(e + 1, 1 - k)
                dve.wait_ge(s_ybfree, e + 1)
                dve.tensor_copy(idx_add[:], idx[:, k, :]).then_inc(s_idadd, 1)
                for j in range(KT):
                    dve.wait_ge(s_dmm, KT * e + (j + 1))
                    dve.tensor_scalar(yb[:, j, :], ps[:, 4 + j % 2, 0:D], gate[:, k, j:j + 1], None, ALU.mult).then_inc(s_y, 1)

            dve.sem_inc(s_y, 2)
            spread(0)
            numbers(0, 0)
            spread(1)
            gates(0, 0)
            with dve.Fori(0, G - 1) as g:
                for k in range(GS):
                    expert(g, k)

            def moments(done, first, row, count):
                if done:
                    dve.wait_ge(s_fmv, done)
                for t in range(count):
                    dve.bn_stats(fst[:, t, :], row(t)).then_inc(s_fst, 1)
                for t in range(count):
                    dve.wait_ge(s_fst, done + t + 1)
                    dve.bn_aggr(fmv[:, first + t, :], fst[:, t, :]).then_inc(s_fmv, 1)

            def block_moments(b, done):
                dve.wait_ge(s_yin[b], 16)
                moments(done, b * TB, lambda t: h_all[:, b * TB + t, 0:D], TB)

            def late_sum(e, j):
                bank = (4, 5, 2, 3)[j] if e == E - 1 else 4 + j % 2
                dve.wait_ge(s_dmm, KT * e + (j + 1))
                dve.scalar_tensor_tensor(out=yb[:, j, :], in0=ps[:, bank, 0:D], scalar=gate[:, e - LATE, j:j + 1],
                                         in1=y_late[:, j, :], op0=ALU.mult, op1=ALU.add).then_inc(s_y, 1)

            numbers(E - 1, 1)
            gates(E - 1, 1)
            dve.wait_ge(s_add, 16 * KT * LATE)
            dve.wait_ge(s_ylate, 16 * KT)
            late_sum(LATE, 0)
            for j in range(1, KT):
                late_sum(LATE, j)
                block_moments(j - 1, (j - 1) * TB)
            block_moments(KT - 1, (KT - 1) * TB)
            dve.wait_ge(s_y, KT * (LATE + 1) + 2)
            moments(KT * TB, NT, lambda t: yb[:, t, :], KT)
            for b in range(KT, NB):
                block_moments(b, b * TB + KT)
            for tile in range(NT - 2 * TB, NT):
                dve.wait_ge(s_frs, tile + KT + 1)
                dve.tensor_scalar(h_all[:, tile, 0:D], h_all[:, tile, 0:D], fmv[:, tile, 0:1], frs[:, tile:tile + 1],
                                  ALU.subtract, ALU.mult).then_inc(s_fin_last, 1)
            dve.wait_ge(s_ylate, 2 * 16 * KT)
            dve.wait_ge(s_fin, NT // 2 + KT)
            for j in range(KT):
                late_sum(E - 1, j)
            dve.wait_ge(s_y, KT * E + 2)
            moments(NT + KT, NT + KT, lambda t: yb[:, t, :], KT)

        @block.scalar
        def _(act):
            def keys(i, j, kind):
                if not has(kind, j, 0):
                    return
                act.wait_ge(s_kx, 4 * i + (j + 3))
                if kind != "first" or j >= 2:
                    act.wait_ge(s_key, 4 * i + (j - 1))
                act.activation(kneg[:, j % 2, :], kx[:, j % 2, :], ACT.Relu, scale=-1.0).then_inc(s_kneg, 1)
                act.wait_ge(s_kneg, 4 * i + (j + 1))
                act.activation(kexp[:, j % 2, :], kneg[:, j % 2, :], ACT.Exp, scale=-1.0).then_inc(s_kexp, 1)

            pair_steps(act, keys)

            def queries(n, m):
                act.wait_ge(s_qmm, C * n + (m + 1))
                act.activation(qrel[:, m, :], ps[:, m, :], ACT.Relu, bias=bq_s[:, m:m + 1])
                act.activation(qexp[:, m, :], ps[:, m, :], ACT.Exp, bias=bq_s[:, m:m + 1]).then_inc(s_qread, 1)

            def tokens(n, t, kind):
                tile = TB * (n - HALF) + t
                first = 0 if has_row(kind, t, 0) else C
                last = 2 * C if has_row(kind, t, 5) else C
                if first < last:
                    act.wait_ge(s_turnmm, tile + 1)
                    act.copy(turned[:, t, first:last, :].rearrange("p c k -> p (c k)"), ps[:, 4, first * P:last * P]).then_inc(s_turned, 1)
                if has_row(kind, t, 4):
                    act.wait_ge(s_shift2, tile - 3)
                    act.wait_ge(s_x1out[t], 32 * (n - HALF))
                    act.activation(x1[:, t, :], us[:, t, :], ACT.Identity, bias=shift2[:, t:t + 1],
                                   scale=rstd2[:, t:t + 1]).then_inc(s_x1, 1)
                if prefetches(kind) and t < C:
                    act.wait_ge(s_q, 2 * n + 2)
                    queries(n + 1, t)

            act.sem_inc(s_turned, 1)
            act.sem_inc(s_x1, TB)
            act.wait_ge(s_wts, 16 * 9)
            for m in range(C):
                queries(0, m)
            tile_steps(act, tokens)

            act.wait_ge(s_soft, 2)
            act.activation(lg[:], prob[:], ACT.Exp).then_inc(s_exp, 1)
            act.activation(spare[:], cs[:, C_PART:C_PART + 1], ACT.Silu).then_inc(s_spare, 1)

            def turn(e):
                act.wait_ge(s_xtmm, e + 1)
                for c in range(C):
                    act.copy(xgt[:, c, :], ps[:, 2 + c, :]).then_inc(s_xt, 1)

            def up(g, e, f):
                width = P if f < FT - 1 else FR
                stand(act, s_umm, FT * e + (f + 1))
                act.activation(mid[0:width, f, :], ps[0:width, f % 2, :], ACT.Silu,
                               bias=bup_s[0:width, bass.ds(g, 1), f:f + 1].rearrange("p a f -> p (a f)")).then_inc(s_mid, 1)

            def expert(g, k, last):
                e = GS * g + k
                for f in range(FT):
                    up(g, e, f)
                if not last:
                    turn(e + 1)

            act.sem_inc(s_mid, 2)
            turn(0)
            with act.Fori(0, G - 1) as g:
                for k in range(GS):
                    expert(g, k, False)

            def normed(done, tile, out_, in_):
                act.wait_ge(s_fnm, done + 1)
                act.activation(out_, in_, ACT.Identity, bias=fnm[:, tile:tile + 1], scale=frs[:, tile:tile + 1]).then_inc(s_fin, 1)

            def normed_row(tile):
                row = h_all[:, tile, 0:D]
                normed(tile + (KT if tile >= NT // 2 else 0), tile, row, row)

            expert(G - 1, 0, False)
            for tile in range(2 * TB):
                normed_row(tile)
            between = [lambda tile=tile: normed_row(tile) for tile in range(2 * TB, 4 * TB)]
            between += [lambda j=j: normed(NT // 2 + j, NT + j, o_late[:, 0, j, :], yb[:, j, :]) for j in range(KT)]
            for f in range(FT):
                up(G - 1, E - 1, f)
                for norm in between[2 * f:2 * f + 2]:
                    norm()
            for tile in range(4 * TB, NT - 2 * TB):
                normed_row(tile)
            for j in range(KT):
                normed(NT + KT + j, NT + KT + j, o_late[:, 1, j, :], yb[:, j, :])

        @block.gpsimd
        def _(pool):
            def tokens(n, t, kind):
                tile = TB * (n - HALF) + t
                if has_row(kind, t, 3):
                    u = (t - 3) % TB
                    pool.wait_ge(s_mv2, tile - 2)
                    pool.tensor_tensor(ve2[:, u:u + 1], mv2[:, u, 1:2], cs[:, C_EPS:C_EPS + 1], ALU.add).then_inc(s_ve2, 1)
                    pool.tensor_tensor(nm[:, u:u + 1], mv2[:, u, 0:1], cs[:, C_NEG:C_NEG + 1], ALU.mult).then_inc(s_nm, 1)
                    pool.wait_ge(s_ve2, tile - 2)
                    pool.tensor_tensor(rstd2[:, u:u + 1], ve2[:, u:u + 1], cs[:, C_HALF:C_HALF + 1], ALU.pow).then_inc(s_rs2, 1)
                    pool.wait_ge(s_nm, tile - 2)
                    pool.wait_ge(s_rs2, tile - 2)
                    pool.tensor_tensor(shift2[:, u:u + 1], nm[:, u:u + 1], rstd2[:, u:u + 1], ALU.mult).then_inc(s_shift2, 1)
                if has_row(kind, t, 1):
                    u = (t - 1) % TB
                    pool.wait_ge(s_mv, tile)
                    pool.tensor_tensor(ve[:, u:u + 1], mv[:, u, 1:2], cs[:, C_EPS:C_EPS + 1], ALU.add).then_inc(s_ve, 1)
                    pool.wait_ge(s_ve, tile)
                    pool.tensor_tensor(rstd[:, u:u + 1], ve[:, u:u + 1], cs[:, C_HALF:C_HALF + 1], ALU.pow).then_inc(s_rs, 1)

            pool.wait_ge(s_wts, 16 * 9)
            tile_steps(pool, tokens)

            for t in range(TB):
                pool.wait_ge(s_x1out[t], 32 * NB + 32)
            pool.wait_ge(s_probout, 16)

            def gather(e, k, slot_used):
                if slot_used:
                    pool.wait_ge(s_xtmm, e)
                    pool.wait_ge(s_gate, e)
                stand(pool, s_idx, e + 1)
                for j in range(KT):
                    pool.indirect_dma_start(out=xg[:, j, :], out_offset=None, in_=table[:, :],
                                            in_offset=bass.IndirectOffsetOnAxis(ap=idx[:, k, j:j + 1], axis=0)).then_inc(s_gat, 16)

            def add_rows(e):
                pool.wait_ge(s_y, KT * e + (KT + 2))
                stand(pool, s_idadd, e + 1)
                for j in range(KT):
                    pool.indirect_dma_start(out=ysum[:, :], out_offset=bass.IndirectOffsetOnAxis(ap=idx_add[:, j:j + 1], axis=0),
                                            in_=yb[:, j, :], in_offset=None, compute_op=ALU.add).then_inc(s_add, 16)

            pool.sem_inc(s_ybfree, 1)
            gather(0, 0, False)
            gather(1, 1, True)
            with pool.Fori(0, G - 1) as g:
                for k in range(GS):
                    e = GS * g + k
                    add_rows(e)
                    gather(e + 2, k, True)
                    pool.wait_ge(s_add, 16 * KT * e + 16 * KT)
                    pool.sem_inc(s_ybfree, 1)

            def factors(done, first, count):
                at = slice(first, first + count)
                pool.wait_ge(s_fmv, done + count)
                pool.tensor_tensor(fve[:, at], fmv[:, at, 1], cs[:, C_EPS:C_EPS + count], ALU.add).then_inc(s_fve, count)
                pool.wait_ge(s_fve, done + count)
                pool.tensor_tensor(frs[:, at], fve[:, at], cs[:, C_HALF:C_HALF + count], ALU.pow).then_inc(s_frs, count)
                pool.wait_ge(s_frs, done + count)
                pool.tensor_tensor(fmr[:, at], fmv[:, at, 0], frs[:, at], ALU.mult).then_inc(s_fmr, count)
                pool.wait_ge(s_fmr, done + count)
                pool.tensor_tensor(fnm[:, at], fmr[:, at], cs[:, C_NEG:C_NEG + count], ALU.mult).then_inc(s_fnm, count)

            def late_rows(k):
                for j in range(KT):
                    pool.indirect_dma_start(out=y_late[:, j, :], out_offset=None, in_=ysum[:, :],
                                            in_offset=bass.IndirectOffsetOnAxis(ap=idx[:, k, j:j + 1], axis=0)).then_inc(s_ylate, 16)

            pool.wait_ge(s_ybfree, LATE + 1)
            late_rows(0)
            for b in range(KT):
                factors(b * TB, b * TB, TB)
            for b in range(NB):
                pool.wait_ge(s_yin[b], 16)
            pool.wait_ge(s_y, KT * (LATE + 1) + 2)
            for j in range(KT):
                pool.indirect_dma_start(out=ysum[:, :], out_offset=bass.IndirectOffsetOnAxis(ap=idx[:, 0, j:j + 1], axis=0),
                                        in_=yb[:, j, :], in_offset=None).then_inc(s_into, 16)
            factors(KT * TB, NT, KT)
            for b in range(KT, NB, 2):
                factors(b * TB + KT, b * TB, 2 * TB)
            pool.wait_ge(s_into, 16 * KT)
            late_rows(1)

            def late_out(k, j):
                pool.wait_ge(s_fin, (NT - 2 * TB + KT if k else NT // 2) + j + 1)
                pool.indirect_dma_start(out=out[:, :], out_offset=bass.IndirectOffsetOnAxis(ap=idx[:, k, j:j + 1], axis=0),
                                        in_=o_late[:, k, j, :], in_offset=None).then_inc(s_late, 16)

            pool.wait_ge(s_out, 16 * NB)
            for j in range(KT):
                late_out(0, j)
            factors(NT + KT, NT + KT, KT)
            pool.wait_ge(s_late, 16 * KT)
            for j in range(KT):
                late_out(1, j)


def kernel(L0_attn_H, L0_attn_W_qkv, L0_attn_b_qkv, L0_attn_W_proj, L0_attn_b_proj, L0_attn_gamma, L0_attn_beta,
           L0_ffn_Wr, L0_ffn_br, L0_ffn_W_up, L0_ffn_b_up, L0_ffn_W_down, L0_ffn_b_down):
    import concourse.bacc as bacc
    from concourse.bass_utils import run_bass_kernel_spmd

    x = np.asarray(L0_attn_H)[0]
    bqkv = np.asarray(L0_attn_b_qkv)
    rows = np.concatenate([bqkv[D:2 * D], L0_attn_b_proj, L0_attn_gamma, L0_attn_beta, L0_ffn_br])
    bup = np.zeros((G, FT * P), np.float32)
    bup[:, :F] = L0_ffn_b_up
    cst, steps = constants()
    xs = x.reshape(PER, 2, P, D).transpose(1, 0, 2, 3).reshape(N, D)
    xq = x.reshape(2, P, PER, D).transpose(0, 2, 1, 3).reshape(N, D)
    ins = {
        "x": xs,
        "xt": xs.T,
        "xtq": xq.T,
        "wqkv": np.asarray(L0_attn_W_qkv).T,
        "bq": bqkv[:D].reshape(C, P).T,
        "bv": bqkv[2 * D:].reshape(1, D),
        "wp": np.asarray(L0_attn_W_proj).T,
        "rows": np.broadcast_to(rows, (P, R_ALL)),
        "wr": np.asarray(L0_ffn_Wr),
        "wup": np.asarray(L0_ffn_W_up),
        "bup": bup.reshape(G, FT, P).transpose(2, 0, 1),
        "wdn": np.concatenate([L0_ffn_W_down, np.asarray(L0_ffn_b_down)[:, None, :]], axis=1),
        "cst": cst,
        "steps": steps,
    }
    nc = bacc.Bacc("TRN2", target_bir_lowering=False, num_devices=1)
    arrays, args = {}, []
    for name, a in ins.items():
        a = np.ascontiguousarray(a)
        arrays[name] = a
        args.append(nc.dram_tensor(name, a.shape, mybir.dt.from_np(a.dtype), kind="ExternalInput").ap())
    args.append(nc.dram_tensor("out", (N, D), F32, kind="ExternalOutput").ap())
    build(nc, *args)
    r = run_bass_kernel_spmd(nc, [arrays], core_ids=[0])
    return r.results[0]["out"].reshape(2, PER, P, D).transpose(1, 0, 2, 3).reshape(1, N, D)
```

```python
from contextlib import ExitStack

import numpy as np

import concourse.bass as bass
from concourse import mybir

P = 128
ALU = mybir.AluOpType
ACT = mybir.ActivationFunctionType
AX = mybir.AxisListType
F32 = mybir.dt.float32
BF16 = mybir.dt.bfloat16
I32 = mybir.dt.int32

N = 4096
D = 256
C = D // P
HEADS = 16
HD = D // HEADS
HH = HEADS // C
TB = 4
BLK = TB * P
NT = N // P
NB = NT // TB
E = 8
GS = 2
G = E // GS
F = int(D * 4 * (2.0 / 3.0))
FT = -(-F // P)
FR = F - (FT - 1) * P
KSEL = N // E
KT = KSEL // P
EPS = 1e-5
ROW = D + E
HC = D + 2
CH = 2 * P
NCH = N // CH
BITS = 30
RB = 2
ROUNDS = BITS // RB
LATE = E - GS
NORMS = NT + GS * KT
CAND = (1 << RB) - 1
HIGH = (BITS - 16) // RB

C_ID, C_HEAD, C_SAME, C_BEFORE, C_IOTA = (P * i for i in range(5))
C_HEAD8 = 5 * P
C_FOUR = C_HEAD8 + HH
C_TILE = C_FOUR + KT
C_PART = C_TILE + NT
C_HALF = C_PART + 1
C_EPS = C_HALF + 2 * TB
C_NEG = C_EPS + 2 * TB
C_PICK = C_NEG + 2 * TB
C_ALL = C_PICK + P
R_BK, R_BP, R_GAMMA, R_BETA = (D * i for i in range(4))
R_BR = 4 * D
R_ALL = R_BR + E
PER = N // 2 // P
PARTS = 3
HALF = PER // TB


def constants():
    p = np.arange(P)
    c = np.zeros((P, C_ALL), np.float32)
    c[:, C_ID:C_ID + P] = np.eye(P)
    c[:, C_HEAD:C_HEAD + P] = p[:, None] // HD == p // HD
    c[:, C_SAME:C_SAME + P] = p[:, None] % E == p % E
    c[:, C_BEFORE:C_BEFORE + P] = (p[:, None] % E == p % E) & (p[:, None] < p)
    c[:, C_IOTA:C_IOTA + P] = p
    c[:, C_HEAD8:C_HEAD8 + HH] = p[:, None] // HD == np.arange(HH)
    c[:, C_FOUR:C_FOUR + KT] = np.arange(KT)
    c[:, C_TILE:C_TILE + NT] = np.arange(NT)
    c[:, C_PART] = p
    c[:, C_HALF:C_HALF + 2 * TB] = -0.5
    c[:, C_EPS:C_EPS + 2 * TB] = EPS
    c[:, C_NEG:C_NEG + 2 * TB] = -1.0
    c[:, C_PICK:C_PICK + P] = ((p % 32 == 0) & (p // 32 < PARTS))[:, None]
    steps = [j << (BITS - RB * (r + 1)) for r in range(ROUNDS) for j in range(1, CAND + 1)]
    return c, np.tile(np.array(steps, np.int32), (P, 1))


def build(nc, x, xt, xtq, wqkv, bq, bv, wp, rows, wr, wup, bup, wdn, cst, steps, out):
    with ExitStack() as ctx:
        def sb(name, shape, dt=F32):
            return ctx.enter_context(nc.sbuf_tensor(name, shape, dt))

        def sem(name):
            return ctx.enter_context(nc.semaphore(name))

        table = nc.dram_tensor("table", [N, ROW], F32, kind="Internal").ap()
        ysum = nc.dram_tensor("ysum", [N, D], F32, kind="Internal").ap()

        ps = ctx.enter_context(nc.psum_tensor("ps", [P, 8, 512], F32))

        cs = sb("cs", [P, C_ALL])
        stp = sb("stp", [P, ROUNDS * CAND], I32)
        rw = sb("rw", [P, R_ALL])
        wqkv_s = sb("wqkv_s", [P, C, 3 * D])
        wp_s = sb("wp_s", [P, C, D])
        wr_s = sb("wr_s", [P, C, E])
        bq_s = sb("bq_s", [P, C])
        bv_s = sb("bv_s", [1, D])
        bup_s = sb("bup_s", [P, G, FT])
        h_all = sb("h_all", [P, NT, HC])
        ht_all = sb("ht_all", [P, C, N])
        heads = sb("heads", [P, NT, D])
        early = heads[:].rearrange("p t d -> p (t d)")
        ht_ring = early[:, 0:2 * C * BLK].rearrange("p (a c n) -> p a c n", a=2, c=C)
        kx, kneg, kexp = (early[:, at * D:(at + 4) * D].rearrange("p (a d) -> p a d", a=2) for at in (8, 12, 16))
        key = early[:, 20 * D:28 * D].rearrange("p (a u d) -> p a u d", a=4, u=2)
        kh = sb("kh", [P, C, HC])
        kht = sb("kht", [P, C, D])
        k1row = sb("k1row", [1, D])
        kvk = sb("kvk", [P, C, P + HH])
        qrel = sb("qrel", [P, C, BLK])
        qexp = sb("qexp", [P, C, BLK])
        qt = sb("qt", [P, C, BLK])
        den = sb("den", [P, TB, HEADS])
        rden = sb("rden", [P, TB, HEADS])
        att = sb("att", [P, TB, D])
        turned = sb("turned", [P, TB, 2 * C, P])
        zg = sb("zg", [P, TB, D])
        st = sb("st", [P, 2, 6])
        mv = sb("mv", [P, TB, 2, 2])
        ve = sb("ve", [P, TB, 2])
        rstd = sb("rstd", [P, TB, 2])
        nm = sb("nm", [P, TB])
        shift2 = sb("shift2", [P, TB])
        us = sb("us", [P, TB, D])
        x1 = sb("x1", [P, TB, D])
        bp_left = sb("bp_left", [P, D])
        bp_parts = sb("bp_parts", [PARTS * 32, D], BF16)
        pick_parts = sb("pick_parts", [PARTS * 32, P], BF16)
        lg = sb("lg", [P, NT, E])
        mx = sb("mx", [P, NT])
        sm = sb("sm", [P, NT])
        prob = sb("prob", [P, NT, E])
        sv = sb("sv", [P, CH])
        cand = sb("cand", [P, CAND], I32)
        thr = sb("thr", [P, 1 + CAND])
        cnt = sb("cnt", [P, CAND], BF16)
        totals = sb("totals", [P, 2], BF16)
        same = sb("same", [P, P], BF16)
        before = sb("before", [P, P], BF16)
        sv_high = sb("sv_high", [P, CH], BF16)
        junk = sb("junk", [P, CAND, CH])
        junk_high = junk[:].rearrange("p a n -> p (a n)")[:, 0:CAND * CH // 2].bitcast(BF16).rearrange("p (a n) -> p a n", n=CH)
        chosen = sb("chosen", [P, CH])
        place = sb("place", [P, CH])
        above = sb("above", [P, CH])
        equal = sb("equal", [P, CH])
        nabove = sb("nabove", [P, CH])
        nequal = sb("nequal", [P, CH])
        capped = junk[:, 0, :]
        taken = junk[:, 1, :]
        ends = sb("ends", [P, 4])
        need = sb("need", [P, 1])
        slot_i = sb("slot_i", [P, CH], I32)
        part_i = sb("part_i", [P, CH], I32)
        part_f = sb("part_f", [P, E, NT], BF16)
        four_i = sb("four_i", [P, CH], I32)
        four_f = sb("four_f", [P, CH])
        dead = ht_all[:].rearrange("p c n -> p (c n)")
        mid = dead[:, 0:FT * KSEL].rearrange("p (f k) -> p f k", f=FT)
        hot = dead[:, FT * KSEL:FT * KSEL + NT * P // 2].bitcast(BF16).rearrange("p (k s) -> p k s", s=NT)
        spare = sb("spare", [P, 1])
        eq4 = sb("eq4", [P, NT, KT])
        pay = sb("pay", [P, NT, 2, KT], BF16)
        idp = sb("idp", [P, 2 * KT])
        idx = sb("idx", [P, 2, KT], I32)
        idx_add = sb("idx_add", [P, KT], I32)
        gate = sb("gate", [P, 2, KT])
        wup_s = sb("wup_s", [P, C, F])
        wdn_s = sb("wdn_s", [P, FT, D])
        xg = sb("xg", [P, KT, ROW])
        xgt = sb("xgt", [P, C, KSEL])
        yb = sb("yb", [P, KT, D])
        y_late = early[:, 0:KT * D].rearrange("p (j d) -> p j d", j=KT)
        y_last = early[:, 6 * KT * D:7 * KT * D].rearrange("p (j d) -> p j d", j=KT)
        o_late = early[:, KT * D:3 * KT * D].rearrange("p (k j d) -> p k j d", k=GS, j=KT)
        stats = early[:, 3 * KT * D:4 * KT * D]
        iotas = early[:, 4 * KT * D:4 * KT * D + P * NT // 2].bitcast(BF16).rearrange("p (k s) -> p k s", s=NT)
        fst = stats[:, 0:TB * 6].rearrange("p (t s) -> p t s", t=TB)
        fmv = stats[:, 32:32 + 2 * NORMS].rearrange("p (t s) -> p t s", s=2)
        fve, frs, fmr, fnm = (stats[:, at:at + NORMS] for at in range(32 + 2 * NORMS, 32 + 6 * NORMS, NORMS))

        s_stood = sem("s_stood")
        s_keyw = sem("s_keyw")
        s_rows = sem("s_rows")
        s_wts = sem("s_wts")
        s_ring = [sem(f"s_ring{i}") for i in range(2)]
        s_h = [sem(f"s_h{i}") for i in range(2)]
        s_ht = sem("s_ht")
        s_x2b = sem("s_x2b")
        s_x2late = sem("s_x2late")
        s_ones = sem("s_ones")
        s_kmm = sem("s_kmm")
        s_kx = sem("s_kx")
        s_kneg = sem("s_kneg")
        s_kexp = sem("s_kexp")
        s_key = sem("s_key")
        s_khmm = sem("s_khmm")
        s_kh = sem("s_kh")
        s_khtmm = sem("s_khtmm")
        s_kht = sem("s_kht")
        s_kvmm = sem("s_kvmm")
        s_kv = sem("s_kv")
        s_qmm = sem("s_qmm")
        s_qread = sem("s_qread")
        s_q = sem("s_q")
        s_amm = sem("s_amm")
        s_den = sem("s_den")
        s_att = sem("s_att")
        s_attin = [sem(f"s_attin{i}") for i in range(TB)]
        s_parts = sem("s_parts")
        s_turnmm = sem("s_turnmm")
        s_turned = sem("s_turned")
        s_zmm = sem("s_zmm")
        s_st = sem("s_st")
        s_st2 = sem("s_st2")
        s_mv = sem("s_mv")
        s_zg = sem("s_zg")
        s_ve = sem("s_ve")
        s_rs = sem("s_rs")
        s_us = sem("s_us")
        s_mv2 = sem("s_mv2")
        s_nm = sem("s_nm")
        s_shift2 = sem("s_shift2")
        s_x1 = sem("s_x1")
        s_x1out = [sem(f"s_x1out{i}") for i in range(TB)]
        s_lmm = sem("s_lmm")
        s_lg = sem("s_lg")
        s_soft = sem("s_soft")
        s_exp = sem("s_exp")
        s_prob = sem("s_prob")
        s_probout = sem("s_probout")
        s_svmm = sem("s_svmm")
        s_thr = sem("s_thr")
        s_kept = sem("s_kept")
        s_cand = sem("s_cand")
        s_high = sem("s_high")
        s_cnt = sem("s_cnt")
        s_tot = sem("s_tot")
        s_sel = sem("s_sel")
        s_pick = sem("s_pick")
        s_pickmm = sem("s_pickmm")
        s_slot = sem("s_slot")
        s_spare = sem("s_spare")
        s_iotas = sem("s_iotas")
        s_wup = sem("s_wup")
        s_wdn = sem("s_wdn")
        s_eq4 = sem("s_eq4")
        s_hot = sem("s_hot")
        s_idmm = sem("s_idmm")
        s_idp = sem("s_idp")
        s_idx = sem("s_idx")
        s_gat = sem("s_gat")
        s_first = [sem(f"s_first{j}") for j in range(KT)]
        s_gate = sem("s_gate")
        s_xtmm = sem("s_xtmm")
        s_xt = sem("s_xt")
        s_umm = sem("s_umm")
        s_mid = sem("s_mid")
        s_midone = sem("s_midone")
        s_dmm = sem("s_dmm")
        s_y = sem("s_y")
        s_idadd = sem("s_idadd")
        s_ybfree = sem("s_ybfree")
        s_add = sem("s_add")
        s_yin = [sem(f"s_yin{i}") for i in range(NB)]
        s_ylate = sem("s_ylate")
        s_into = sem("s_into")
        s_fst = sem("s_fst")
        s_fmv = sem("s_fmv")
        s_fve = sem("s_fve")
        s_frs = sem("s_frs")
        s_fmr = sem("s_fmr")
        s_fnm = sem("s_fnm")
        s_fin = sem("s_fin")
        s_fin_last = sem("s_fin_last")
        s_out = sem("s_out")
        s_late = sem("s_late")

        ident = cs[:, C_ID:C_ID + P]
        table_t = table.rearrange("(s p) c -> p s c", p=P)
        ysum_t = ysum.rearrange("(s p) c -> p s c", p=P)
        out_t = out.rearrange("(s p) c -> p s c", p=P)
        x_t = x.rearrange("(s p) c -> p s c", p=P)
        xt_t = xt.rearrange("(c p) n -> p c n", p=P)
        xtq_t = xtq.rearrange("(c p) n -> p c n", p=P)

        block = ctx.enter_context(nc.Block())

        def pair_steps(eng, step):
            for j in range(4):
                step(0, j, "first")
            with eng.Fori(1, NB // 2 - 1) as i:
                for j in range(4):
                    step(i, j, "loop")
            for j in range(4):
                step(NB // 2 - 1, j, "last")
            for j in range(2):
                step(NB // 2, j, "drain")

        def tile_steps(eng, step):
            for kind, begin, end in (("attend", 0, HALF), ("begin", HALF, HALF + 1),
                                     ("second", HALF + 1, HALF + 2), ("both", HALF + 2, NB - 1),
                                     ("attended", NB - 1, NB), ("again", NB, NB + 1), ("rows", NB + 1, NB + HALF - 1),
                                     ("last", NB + HALF - 1, NB + HALF), ("drain", NB + HALF, NB + HALF + 1),
                                     ("end", NB + HALF + 1, NB + HALF + 2)):
                if end - begin == 1:
                    for t in range(TB):
                        step(begin, t, kind)
                else:
                    with eng.Fori(begin, end) as n:
                        for t in range(TB):
                            step(n, t, kind)

        def attends(kind):
            return kind in ("attend", "begin", "second", "both", "attended")

        def prefetches(kind):
            return kind in ("attend", "begin", "second", "both")

        def has_row(kind, t, lag):
            return {"attend": False, "begin": t >= lag, "second": TB + t >= lag,
                    "drain": t < lag, "end": TB + t < lag}.get(kind, True)

        def stand(eng, semaphore, value):
            eng.wait_ge(semaphore, value)
            eng.sem_inc(s_stood, 1)

        def has(kind, t, lag):
            return {"first": t >= lag, "drain": t < lag}.get(kind, True)

        @block.sync
        def _(sp):
            sp.dma_start(wqkv_s[:, :, D:2 * D], wqkv.rearrange("(c p) e -> p c e", p=P)[:, :, D:2 * D]).then_inc(s_keyw, 16)
            def load_block(i, half):
                b = 2 * i + half
                cols = bass.ds(b * BLK, BLK)
                sp.dma_start(ht_ring[:, half], xt_t[:, :, cols]).then_inc(s_ring[half], 16)
                sp.dma_start(h_all[:, bass.ds(b * TB, TB), 0:D], x_t[:, bass.ds(b * TB, TB), :]).then_inc(s_h[half], 16)

            sp.dma_start(ht_ring[:, 0], xt_t[:, :, 0:BLK]).then_inc(s_ring[0], 16)
            sp.dma_start(rw[:], rows).then_inc(s_rows, 16)
            sp.dma_start(h_all[:, 0:TB, 0:D], x_t[:, 0:TB, :]).then_inc(s_h[0], 16)
            load_block(0, 1)
            sp.dma_start(cs[:], cst).then_inc(s_wts, 16)
            sp.dma_start(stp[:], steps).then_inc(s_wts, 16)
            for half in (0, 1):
                sp.dma_start(wqkv_s[:, :, 2 * D * half:2 * D * half + D],
                             wqkv.rearrange("(c p) e -> p c e", p=P)[:, :, 2 * D * half:2 * D * half + D]).then_inc(s_wts, 16)
            sp.dma_start(wp_s[:], wp.rearrange("(c p) e -> p c e", p=P)).then_inc(s_wts, 16)
            sp.dma_start(wr_s[:], wr.rearrange("(c p) e -> p c e", p=P)).then_inc(s_wts, 16)
            sp.dma_start(bq_s[:], bq).then_inc(s_wts, 16)
            sp.dma_start(bv_s[:], bv).then_inc(s_wts, 16)
            sp.dma_start(bup_s[:], bup).then_inc(s_wts, 16)
            def load_queries(b):
                cols = bass.ds(b * BLK, BLK)
                sp.dma_start(ht_all[:, :, cols], xtq_t[:, :, cols]).then_inc(s_ht, 16)

            with sp.Fori(1, NB // 2) as i:
                for half in range(2):
                    stand(sp, s_kmm, 4 * i + (2 * half - 2))
                    stand(sp, s_h[half], 16 * i)
                    load_block(i, half)
            load_queries(0)
            with sp.Fori(1, NB) as b:
                stand(sp, s_ht, 16 * b)
                load_queries(b)

            def load_up(g):
                sp.dma_start(wup_s[:], wup[bass.ds(g, 1)].rearrange("g (c p) f -> p (g c) f", p=P)).then_inc(s_wup, 16)

            def load_down(e):
                full = (FT - 1) * P
                sp.dma_start(wdn_s[:, 0:FT - 1, :],
                             wdn[bass.ds(e, 1), 0:full, :].rearrange("g (f p) d -> p (g f) d", p=P)).then_inc(s_wdn, 16)
                sp.dma_start(wdn_s[0:FR + 1, FT - 1:FT, :],
                             wdn[bass.ds(e, 1), full:F + 1, :].rearrange("g p d -> p g d")).then_inc(s_wdn, 16)

            load_up(0)
            load_down(0)

            def store(m, u):
                stand(sp, s_x1, TB * m + (u + 1 + TB))
                tile = TB * m + u
                sp.dma_start(table_t[:, bass.ds(tile, 1), 0:D], x1[:, u:u + 1, :]).then_inc(s_x1out[u], 16)
                sp.dma_start(ysum_t[:, bass.ds(tile, 1), :], x1[:, u:u + 1, :]).then_inc(s_x1out[u], 16)

            def regroup(row, t):
                sp.dma_start(att[:, t % TB:t % TB + 1, :], heads[:, bass.ds(row, 1), :]).then_inc(s_attin[t % TB], 16)

            def move(n, t, kind):
                row = TB * (n - HALF) + t
                if has_row(kind, t, 4):
                    store(n - HALF - 1, t)
                if has_row(kind, t, 0) and not (kind in ("begin", "again") if t == 0 else kind in ("attended", "last")):
                    if t == 1 and kind in ("begin", "again"):
                        sp.wait_ge(s_att, (PER if kind == "begin" else NT) + 2)
                    stand(sp, s_turnmm, row)
                    regroup(row + 3, t + 3)

            for t in range(TB):
                sp.sem_inc(s_x1out[t], 32)
            tile_steps(sp, move)
            sp.wait_ge(s_prob, 1)
            with nc.allow_non_contiguous_dma(reason="eight probabilities a token"):
                sp.dma_start(table_t[:, :, D:ROW], prob[:]).then_inc(s_probout, 16)
            for e in range(1, GS):
                sp.wait_ge(s_dmm, KT * e)
                load_down(e)
            with sp.Fori(1, G - 1) as g:
                stand(sp, s_umm, GS * FT * g)
                load_up(g)
                for k in range(GS):
                    stand(sp, s_dmm, GS * KT * g + KT * k)
                    load_down(GS * g + k)
            sp.wait_ge(s_umm, FT * LATE)
            load_up(G - 1)
            sp.wait_ge(s_dmm, KT * LATE)
            load_down(LATE)
            sp.wait_ge(s_ybfree, LATE + 1)
            sp.wait_ge(s_gat, 16 * KT * (E - 1))
            sp.wait_ge(s_ylate, 16 * KT)
            for b in range(NB):
                tiles = slice(b * TB, (b + 1) * TB)
                sp.dma_start(h_all[:, tiles, 0:D], ysum_t[:, tiles, :]).then_inc(s_yin[b], 16)

            def store_block(b):
                tiles = slice(b * TB, (b + 1) * TB)
                sp.dma_start(out_t[:, tiles, :], h_all[:, tiles, 0:D]).then_inc(s_out, 16)

            for b in range(2):
                sp.wait_ge(s_fin, TB * (b + 1))
                store_block(b)
            sp.wait_ge(s_dmm, KT * (E - 1))
            load_down(E - 1)
            for b in range(2, NB // 2):
                sp.wait_ge(s_fin, TB * (b + 1))
                store_block(b)
            for b in range(NB // 2, NB - 2):
                sp.wait_ge(s_fin, TB * (b + 1))
                store_block(b)
            for b in range(NB - 2, NB):
                sp.wait_ge(s_fin_last, TB * (b - NB + 3))
                store_block(b)
            sp.wait_ge(s_late, 16 * GS * KT)

        @block.tensor
        def _(pe):
            def keys(i, j, kind):
                bank = j % 2
                if has(kind, j, 0):
                    if j % 2 == 0:
                        pe.wait_ge(s_ring[j // 2], 16 * i + 16)
                    pe.wait_ge(s_kx, 4 * i + (j + 1))
                    for u in range(2):
                        for c in range(C):
                            at = (2 * (j % 2) + u) * P
                            mm = pe.matmul(ps[:, bank, u * D:(u + 1) * D], ht_ring[:, j // 2, c, at:at + P],
                                           wqkv_s[:, c, D:2 * D], start=(c == 0), stop=(c == C - 1))
                    mm.then_inc(s_kmm, 1)
                if has(kind, j, 2):
                    back = j - 2
                    pe.wait_ge(s_key, 4 * i + (back + 1))
                    if j % 2 == 0:
                        if j == 0:
                            pe.wait_ge(s_h[1], 16 * i)
                        else:
                            pe.wait_ge(s_h[0], 16 * i + 16)
                    for u in range(2):
                        for c in range(C):
                            begins = kind == "first" and back == 0 and u == 0
                            ends_ = kind == "drain" and j == 1 and u == 1
                            mm = pe.matmul(ps[:, 2 + c, 0:HC], key[:, back % 4, u, c * P:(c + 1) * P],
                                           h_all[:, bass.ds(i * 8 + (2 * back + u), 1), :].rearrange("p a h -> p (a h)"),
                                           start=begins, stop=ends_, skip_group_check=True)
                    mm.then_inc(s_khmm, 1)

            def queries(n, m):
                for c in range(C):
                    mm = pe.matmul(ps[:, m, :], wqkv_s[:, c, m * P:(m + 1) * P], ht_all[:, c, bass.ds(n * BLK, BLK)],
                                   start=(c == 0), stop=(c == C - 1))
                mm.then_inc(s_qmm, 1)

            pe.wait_ge(s_keyw, 16)
            pe.wait_ge(s_ones, 1)
            pair_steps(pe, keys)

            pe.wait_ge(s_wts, 16 * 9)
            pe.wait_ge(s_kx, NT // 2 + 2)
            pe.wait_ge(s_ht, 16)
            for m in range(C):
                queries(0, m)

            pe.wait_ge(s_kh, 2)
            for c in range(C):
                for h in range(C):
                    pe.transpose(ps[:, 4, h * D + c * P:h * D + (c + 1) * P], kh[:, c, h * P:(h + 1) * P], ident)
            for c in range(C):
                mm = pe.transpose(ps[0:1, 5, c * P:(c + 1) * P], kh[:, c, D:D + 1], ident)
            mm.then_inc(s_khtmm, 1)
            pe.wait_ge(s_kht, 2)
            for c in range(C):
                half = slice(c * P, (c + 1) * P)
                for h in range(C):
                    pe.matmul(ps[:, 6, half], kht[:, h, half], wqkv_s[:, h, 2 * D + c * P:2 * D + (c + 1) * P],
                              start=(h == 0), stop=False)
                mm = pe.matmul(ps[:, 6, half], k1row[:, half], bv_s[:, half], start=False, stop=True)
            mm.then_inc(s_kvmm, 1)

            def turn_tiles(n, t, kind):
                row = TB * (n - HALF) + t
                turns = 0
                if has_row(kind, t, 0) or has_row(kind, t, 5):
                    pe.wait_ge(s_turned, row + 1)
                if has_row(kind, t, 0):
                    if kind in ("begin", "again"):
                        pe.wait_ge(s_att, (PER if kind == "begin" else NT) + 2)
                        source = heads[:, row, :]
                    else:
                        pe.wait_ge(s_attin[t], 16 * (n - HALF) - (16 if kind in ("rows", "last") else 0))
                        source = att[:, t, :]
                    for c in range(C):
                        mm = pe.transpose(ps[:, 4, c * P:(c + 1) * P], source[:, c * P:(c + 1) * P], ident)
                    turns = 1
                if has_row(kind, t, 5):
                    pe.wait_ge(s_x1, row - 4 + TB)
                    for c in range(C):
                        mm = pe.transpose(ps[:, 4, D + c * P:D + (c + 1) * P], x1[:, (t - 5) % TB, c * P:(c + 1) * P], ident)
                    turns = 1
                if turns:
                    mm.then_inc(s_turnmm, 1)

            def tokens(n, t, kind):
                row = TB * (n - HALF) + t
                if attends(kind):
                    if t % 2 == 0:
                        pe.wait_ge(s_q, 2 * n + (t // 2 + 1))
                    pe.wait_ge(s_att, TB * n + (t + 1))
                    for c in range(C):
                        mm = pe.matmul(ps[:, 2 + t % 2, c * (P + HH):(c + 1) * (P + HH)], qt[:, c, t * P:(t + 1) * P],
                                       kvk[:, c, :], start=True, stop=True)
                    mm.then_inc(s_amm, 1)
                if not (kind == "begin" and t == 0):
                    turn_tiles(n, t, kind)
                if has_row(kind, t, 6):
                    pe.wait_ge(s_turned, row + 1)
                    for c in range(C):
                        mm = pe.matmul(ps[:, 7, bass.ds((row - 6) * E, E)], turned[:, (t - 1) % TB, C + c, :], wr_s[:, c, :],
                                       start=(c == 0), stop=(c == C - 1))
                    mm.then_inc(s_lmm, 1)
                if has_row(kind, t, 1):
                    pe.wait_ge(s_turned, row + 1)
                    pe.wait_ge(s_zg, row)
                    bank = ps[:, 5 + (t - 1) % 2, 0:D]
                    pe.matmul(bank, pick_parts[:], bp_parts[:], start=True, stop=False)
                    for c in range(C):
                        mm = pe.matmul(bank, turned[:, (t - 1) % TB, c, :], wp_s[:, c, :], start=False, stop=(c == C - 1))
                    mm.then_inc(s_zmm, 1)
                if prefetches(kind) and t < C:
                    pe.wait_ge(s_qread, C * n + (t + 1))
                    if t == 0:
                        pe.wait_ge(s_ht, 16 * n + 32)
                    queries(n + 1, t)
                if kind == "begin" and t == 0:
                    turn_tiles(n, t, kind)

            pe.wait_ge(s_kv, 1)
            pe.wait_ge(s_parts, 8)
            tile_steps(pe, tokens)

            pe.wait_ge(s_prob, 1)
            for h in range(2):
                mm = pe.transpose(ps[:, 0, h * P:(h + 1) * P], prob[:, h * NCH:(h + 1) * NCH, :].rearrange("p i e -> p (i e)"), ident)
            mm.then_inc(s_svmm, 1)
            with pe.Fori(0, ROUNDS // 5) as turn:
                for k in range(5):
                    pe.wait_ge(s_cnt, 5 * turn + (k + 1))
                    pe.matmul(ps[:, 1, 0:CAND], same[:], cnt[:], start=True, stop=True).then_inc(s_tot, 1)
            pe.wait_ge(s_sel, 1)
            pe.matmul(ps[:, 1, 0:1], same[:], totals[:, 0:1], start=True, stop=True)
            pe.matmul(ps[:, 1, 1:3], before[:], totals[:], start=True, stop=True).then_inc(s_tot, 1)
            pe.wait_ge(s_pick, 11)
            for h in range(2):
                mm = pe.transpose(ps[:, 0, h * P:(h + 1) * P], place[:, h * P:(h + 1) * P], ident)
            mm.then_inc(s_pickmm, 1)

            def lists(e):
                pe.wait_ge(s_hot, e + 1)
                for s in range(NT):
                    mm = pe.matmul(ps[:, 6, 0:2 * KT], hot[:, :, s], pay[:, s].rearrange("p w k -> p (w k)"),
                                   start=(s == 0), stop=(s == NT - 1))
                mm.then_inc(s_idmm, 1)

            def turn(e, first=False):
                if not first:
                    pe.wait_ge(s_gat, 16 * KT * e)
                for k in range(KT):
                    if first:
                        pe.wait_ge(s_first[k], 16)
                    for c in range(C):
                        mm = pe.transpose(ps[:, 2 + c, k * P:(k + 1) * P], xg[:, k, c * P:(c + 1) * P], ident)
                mm.then_inc(s_xtmm, 1)

            def expert(g, k, last):
                e = GS * g + k
                if not last:
                    lists(e + 1)
                pe.wait_ge(s_xt, C * e + C)
                if k == 0:
                    pe.wait_ge(s_wup, 16 * g + 16)
                for f in range(FT):
                    width = P if f < FT - 1 else FR
                    pe.wait_ge(s_mid, e * FT + (f + 1))
                    for c in range(C):
                        mm = pe.matmul(ps[0:width, f % 2, :], wup_s[:, c, f * P:f * P + width], xgt[:, c, :],
                                       start=(c == 0), stop=(c == C - 1))
                    mm.then_inc(s_umm, 1)
                if not last:
                    turn(e + 1)
                pe.wait_ge(s_wdn, 32 * e + 32)
                for j in range(KT):
                    if last:
                        bank = (4, 5, 2, 3)[j]
                    else:
                        bank = 4 + j % 2
                    if not last or j < 2:
                        pe.wait_ge(s_y, e * KT + (j + 1))
                    for f in range(FT):
                        rows_ = P if f < FT - 1 else FR + 1
                        if j == 0:
                            pe.wait_ge(s_mid, e * FT + (f + 3))
                        mm = pe.matmul(ps[:, bank, 0:D], mid[0:rows_, f, j * P:(j + 1) * P], wdn_s[0:rows_, f, :],
                                       start=(f == 0), stop=(f == FT - 1))
                    mm.then_inc(s_dmm, 1)

            lists(0)
            turn(0, True)
            pe.wait_ge(s_midone, 1)
            with pe.Fori(0, G - 1) as g:
                for k in range(GS):
                    expert(g, k, False)
            for k in range(GS):
                expert(G - 1, k, k == GS - 1)

        @block.vector
        def _(dve):
            dve.memset(h_all[:, :, D:HC], 1.0).then_inc(s_ones, 1)
            dve.sem_inc(s_kx, 2)

            def keys(i, j, kind):
                if has(kind, j, 0):
                    dve.wait_ge(s_kmm, 4 * i + (j + 1))
                    if kind != "first" or j >= 2:
                        dve.wait_ge(s_key, 4 * i + (j - 1))
                    dve.tensor_tensor(kx[:, j % 2, :].rearrange("p (u d) -> p u d", u=2),
                                      ps[:, j % 2, :].rearrange("p (u d) -> p u d", u=2),
                                      rw[:, R_BK:R_BK + D].unsqueeze(1).to_broadcast([P, 2, D]), ALU.add).then_inc(s_kx, 1)
                if has(kind, j, 1):
                    dve.wait_ge(s_kexp, 4 * i + j)
                    b = (j - 1) % 2
                    dve.scalar_tensor_tensor(out=key[:, (j - 1) % 4].rearrange("p u d -> p (u d)"), in0=kx[:, b, :], scalar=0.0,
                                             in1=kexp[:, b, :], op0=ALU.max, op1=ALU.add).then_inc(s_key, 1)
                if kind in ("loop", "last"):
                    double(4 * i + (j - 4))

            def double(pair):
                dve.wait_ge(s_khmm, pair + 1)
                tiles = h_all[:, bass.ds(2 * pair, 2), 0:D]
                dve.scalar_tensor_tensor(out=tiles, in0=tiles, scalar=2.0,
                                         in1=rw[:, R_BETA:R_BETA + D].unsqueeze(1).to_broadcast([P, 2, D]),
                                         op0=ALU.mult, op1=ALU.add).then_inc(s_x2b, 1)

            dve.wait_ge(s_rows, 16)
            dve.tensor_copy(bp_parts[:], rw[0:PARTS * 32, R_BP:R_BP + D]).then_inc(s_parts, 1)
            done = 1
            for part in range(1, PARTS):
                at = slice(32 * part, 32 * part + 32)
                src = rw[at, R_BP:R_BP + D]
                for _ in range(part):
                    dve.wait_ge(s_parts, done)
                    dve.tensor_tensor(bp_left[at, :], src, bp_parts[at, :], ALU.subtract).then_inc(s_parts, 1)
                    dve.wait_ge(s_parts, done + 1)
                    dve.tensor_copy(bp_parts[at, :], bp_left[at, :]).then_inc(s_parts, 1)
                    src = bp_left[at, :]
                    done += 2
            pair_steps(dve, keys)

            def make_q(n, half):
                cols = slice(half * BLK // 2, (half + 1) * BLK // 2)
                if half == 0:
                    dve.wait_ge(s_qread, C * n + C)
                dve.scalar_tensor_tensor(out=qt[:, :, cols], in0=qexp[:, :, cols], scalar=1.0, in1=qrel[:, :, cols],
                                         op0=ALU.min, op1=ALU.add).then_inc(s_q, 1)

            dve.wait_ge(s_khmm, NT // 2)
            for c in range(C):
                dve.tensor_copy(kh[:, c, :], ps[:, 2 + c, 0:HC]).then_inc(s_kh, 1)
            dve.wait_ge(s_kh, 2)
            dve.wait_ge(s_wts, 16 * 9)
            for c in range(C):
                dve.tensor_scalar(kvk[:, c, P:P + HH], cs[:, C_HEAD8:C_HEAD8 + HH], kh[:, c, D:D + 1], None, ALU.mult)
            dve.wait_ge(s_khtmm, 1)
            dve.tensor_copy(kht[:].rearrange("p c d -> p (c d)"), ps[:, 4, :]).then_inc(s_kht, 1)
            dve.tensor_copy(k1row[:], ps[0:1, 5, 0:D]).then_inc(s_kht, 1)
            make_q(0, 0)
            make_q(0, 1)
            dve.wait_ge(s_kvmm, 1)
            dve.tensor_tensor(kvk[:, :, 0:P], ps[:, 6, 0:D].rearrange("p (c v) -> p c v", c=C),
                              cs[:, C_HEAD:C_HEAD + P].unsqueeze(1).to_broadcast([P, C, P]), ALU.mult).then_inc(s_kv, 1)
            dve.tensor_copy(pick_parts[:], cs[0:PARTS * 32, C_PICK:C_PICK + P]).then_inc(s_parts, 1)
            dve.tensor_copy(same[:], cs[:, C_SAME:C_SAME + P])
            dve.tensor_copy(before[:], cs[:, C_BEFORE:C_BEFORE + P])
            dve.memset(thr[:], 0.0).then_inc(s_thr, 1)

            def tokens(n, t, kind):
                tile = TB * (n - HALF) + t
                if has_row(kind, t, 3):
                    u = (t - 3) % TB
                    dve.wait_ge(s_rs, tile - 2)
                    dve.wait_ge(s_zg, tile)
                    dve.wait_ge(s_x1, tile - 2)
                    if kind == "begin":
                        dve.wait_ge(s_x2b, NT // 2 - 4)
                        dve.wait_ge(s_x2late, 8)
                    dve.scalar_tensor_tensor(out=us[:, u, :], in0=zg[:, u, :], scalar=rstd[:, (t - 2) % TB, 0:1],
                                             in1=h_all[:, bass.ds(tile - 3, 1), 0:D].rearrange("p a d -> p (a d)"),
                                             op0=ALU.mult, op1=ALU.add).then_inc(s_us, 1)
                    dve.wait_ge(s_us, tile - 2)
                    dve.bn_stats(st[:, 1, :], us[:, u, :]).then_inc(s_st2, 1)
                if attends(kind):
                    dve.wait_ge(s_amm, TB * n + (t + 1))
                    bank = ps[:, 2 + t % 2, 0:C * (P + HH)].rearrange("p (c w) -> p c w", c=C)
                    dve.tensor_scalar(den[:, t].rearrange("p (c h) -> p c h", c=C), bank[:, :, P:P + HH], 1e-6, None,
                                      ALU.max).then_inc(s_den, 1)
                    dve.wait_ge(s_den, 2 * TB * n + (2 * t + 1))
                    dve.reciprocal(rden[:, t, :], den[:, t, :]).then_inc(s_den, 1)
                if has_row(kind, t, 1):
                    u = (t - 1) % TB
                    z_bank = ps[:, 5 + u % 2, 0:D]
                    dve.wait_ge(s_zmm, tile)
                    dve.bn_stats(st[:, 0, :], z_bank).then_inc(s_st, 1)
                if has_row(kind, t, 3):
                    stand(dve, s_st2, tile - 2)
                    dve.bn_aggr(mv[:, t, 1, :], st[:, 1, :]).then_inc(s_mv2, 1)
                if has_row(kind, t, 1):
                    stand(dve, s_st, tile)
                    dve.bn_aggr(mv[:, t, 0, :], st[:, 0, :]).then_inc(s_mv, 1)
                if attends(kind):
                    w = 0 if kind == "attend" else 1
                    j = bass.ds(TB * (n - HALF * w) + t, 1)
                    dve.wait_ge(s_den, 2 * TB * n + (2 * t + 2))
                    dve.tensor_tensor(heads[:, PER * w:PER * (w + 1), :].rearrange("p (c h) (j d) -> p c h j d", c=C, j=PER)[:, :, :, j, :].rearrange("p c h j d -> p c h (j d)"),
                                      bank[:, :, 0:P].rearrange("p c (h d) -> p c h d", h=HH),
                                      rden[:, t, :].rearrange("p (c h) -> p c h", c=C).unsqueeze(3).to_broadcast([P, C, HH, HD]),
                                      ALU.mult).then_inc(s_att, 1)
                if prefetches(kind) and t >= TB // 2:
                    make_q(n + 1, t - TB // 2)
                if has_row(kind, t, 1):
                    dve.wait_ge(s_mv, tile)
                    dve.scalar_tensor_tensor(out=zg[:, u, :], in0=z_bank, scalar=mv[:, t, 0, 0:1], in1=rw[:, R_GAMMA:R_GAMMA + D],
                                             op0=ALU.subtract, op1=ALU.mult).then_inc(s_zg, 1)

            dve.sem_inc(s_att, 2)
            dve.sem_inc(s_zg, 2)
            tile_steps(dve, tokens)

            wide = [P, NT, E]
            dve.wait_ge(s_lmm, NT)
            dve.tensor_tensor(lg[:], ps[:, 7, 0:NT * E].rearrange("p (s e) -> p s e", e=E),
                              rw[:, R_BR:R_BR + E].unsqueeze(1).to_broadcast([P, NT, E]), ALU.add).then_inc(s_lg, 1)
            dve.wait_ge(s_lg, 1)
            dve.tensor_reduce(mx[:], lg[:], AX.X, ALU.max).then_inc(s_soft, 1)
            dve.wait_ge(s_soft, 1)
            dve.tensor_tensor(prob[:], lg[:], mx[:].unsqueeze(2).to_broadcast(wide), ALU.subtract).then_inc(s_soft, 1)
            dve.memset(mid[0:64, FT - 1, :], 1.0).then_inc(s_midone, 1)
            dve.wait_ge(s_exp, 1)
            dve.tensor_reduce(sm[:], lg[:], AX.X, ALU.add).then_inc(s_soft, 1)
            dve.wait_ge(s_soft, 3)
            dve.reciprocal(mx[:], sm[:]).then_inc(s_soft, 1)
            dve.wait_ge(s_soft, 4)
            dve.tensor_tensor(prob[:], lg[:], mx[:].unsqueeze(2).to_broadcast(wide), ALU.mult).then_inc(s_prob, 1)

            dve.wait_ge(s_svmm, 1)
            dve.tensor_copy(sv[:], ps[:, 0, 0:CH]).then_inc(s_high, 1)
            dve.wait_ge(s_high, 1)
            dve.tensor_copy(sv_high[:], sv[:].bitcast(BF16).rearrange("p (n h) -> p n h", h=2)[:, :, 1]).then_inc(s_cand, 1)
            def search(r, values, out_):
                dve.wait_ge(s_thr, r + 1)
                dve.tensor_tensor(cand[:], thr[:, 0:1].bitcast(I32).to_broadcast([P, CAND]), stp[:, bass.ds(r * CAND, CAND)],
                                  ALU.bitwise_or).then_inc(s_cand, 1)
                dve.wait_ge(s_cand, r + 2)
                for q in range(CAND):
                    last = dve.tensor_scalar(out_[:, q, :], values, cand[:, q:q + 1].bitcast(F32), 0.0, ALU.is_ge, ALU.add,
                                             accum_out=cnt[:, q:q + 1])
                last.then_inc(s_cnt, 1)
                dve.wait_ge(s_tot, r + 1)
                dve.scalar_tensor_tensor(out=thr[:, 1:1 + CAND], in0=ps[:, 1, 0:CAND], scalar=KSEL - 0.5,
                                         in1=cand[:].bitcast(F32), op0=ALU.is_ge, op1=ALU.mult).then_inc(s_kept, 1)
                dve.wait_ge(s_kept, r + 1)
                dve.tensor_reduce(thr[:, 0:1], thr[:], AX.X, ALU.max).then_inc(s_thr, 1)

            for r in range(HIGH):
                search(r, sv_high[:], junk_high)
            with dve.Fori(0, (ROUNDS - HIGH) // 4) as turn:
                for k in range(4):
                    search(4 * turn + (k + HIGH), sv[:], junk)
            dve.wait_ge(s_thr, ROUNDS + 1)
            dve.tensor_scalar(above[:], sv[:], thr[:, 0:1], 0.0, ALU.is_gt, ALU.add, accum_out=totals[:, 0:1]).then_inc(s_pick, 1)
            dve.tensor_scalar(equal[:], sv[:], thr[:, 0:1], 0.0, ALU.is_equal, ALU.add, accum_out=totals[:, 1:2]).then_inc(s_sel, 1)
            dve.wait_ge(s_pick, 1)
            dve.tensor_tensor_scan(nabove[:], above[:], above[:], 0.0, ALU.add, ALU.max).then_inc(s_pick, 1)
            dve.wait_ge(s_sel, 1)
            dve.tensor_tensor_scan(nequal[:], equal[:], equal[:], 0.0, ALU.add, ALU.max).then_inc(s_pick, 1)
            dve.wait_ge(s_tot, ROUNDS + 1)
            dve.tensor_copy(ends[:, 0:3], ps[:, 1, 0:3]).then_inc(s_pick, 1)
            dve.wait_ge(s_pick, 4)
            dve.tensor_scalar(ends[:, 3:4], ends[:, 0:1], -1.0, float(KSEL), ALU.mult, ALU.add).then_inc(s_pick, 1)
            dve.wait_ge(s_pick, 5)
            dve.tensor_tensor(need[:], ends[:, 3:4], ends[:, 2:3], ALU.subtract).then_inc(s_pick, 1)
            dve.tensor_scalar(capped, nequal[:], ends[:, 2:3], ends[:, 3:4], ALU.add, ALU.min).then_inc(s_pick, 1)
            dve.wait_ge(s_pick, 6)
            dve.scalar_tensor_tensor(out=taken, in0=nequal[:], scalar=need[:, 0:1], in1=equal[:],
                                     op0=ALU.is_le, op1=ALU.mult).then_inc(s_pick, 1)
            dve.wait_ge(s_pick, 7)
            dve.scalar_tensor_tensor(out=place[:], in0=nabove[:], scalar=ends[:, 1:2], in1=capped,
                                     op0=ALU.add, op1=ALU.add).then_inc(s_pick, 1)
            dve.wait_ge(s_pick, 8)
            dve.tensor_tensor(chosen[:], taken, above[:], ALU.add).then_inc(s_pick, 1)
            dve.wait_ge(s_pick, 10)
            dve.tensor_tensor(place[:], place[:], chosen[:], ALU.mult).then_inc(s_pick, 1)
            dve.wait_ge(s_pickmm, 1)
            dve.tensor_scalar(slot_i[:], ps[:, 0, 0:CH], -1.0, None, ALU.add).then_inc(s_slot, 1)
            dve.wait_ge(s_slot, 1)
            dve.tensor_scalar(part_i[:], slot_i[:], KT.bit_length() - 1, None, ALU.arith_shift_right).then_inc(s_slot, 1)
            dve.tensor_scalar(four_i[:], slot_i[:], KT - 1, None, ALU.bitwise_and).then_inc(s_slot, 1)
            dve.wait_ge(s_slot, 3)
            dve.tensor_copy(part_f[:], part_i[:].rearrange("p (s e) -> p e s", e=E)).then_inc(s_slot, 1)
            dve.tensor_copy(four_f[:], four_i[:]).then_inc(s_slot, 1)
            dve.wait_ge(s_slot, 5)

            def spread(e):
                shape = [P, NT, KT]
                part = part_f[:, bass.ds(e, 1), :]
                four = four_f[:].rearrange("p (s e) -> p s e", e=E)[:, :, bass.ds(e, 1)]
                dve.tensor_tensor(eq4[:], four.to_broadcast(shape),
                                  cs[:, C_FOUR:C_FOUR + KT].unsqueeze(1).to_broadcast(shape), ALU.is_equal).then_inc(s_eq4, 1)
                dve.wait_ge(s_eq4, e + 1)
                dve.tensor_tensor(pay[:, :, 0, :], eq4[:], cs[:, C_TILE:C_TILE + NT].unsqueeze(2).to_broadcast(shape), ALU.mult)
                dve.tensor_scalar(pay[:, :, 1, :], eq4[:], cs[:, C_PART:C_PART + 1], None, ALU.mult)
                dve.tensor_tensor(hot, part.to_broadcast([P, P, NT]), iotas, ALU.is_equal).then_inc(s_hot, 1)

            def numbers(e, k):
                dve.wait_ge(s_idmm, e + 1)
                dve.tensor_copy(idp[:], ps[:, 6, 0:2 * KT]).then_inc(s_idp, 1)
                dve.wait_ge(s_idp, e + 1)
                dve.scalar_tensor_tensor(out=idx[:, k, :], in0=idp[:, 0:KT], scalar=float(P), in1=idp[:, KT:2 * KT],
                                         op0=ALU.mult, op1=ALU.add).then_inc(s_idx, 1)

            def gates(e, k, first=False):
                if first:
                    for j in range(KT):
                        dve.wait_ge(s_first[j], 16)
                else:
                    dve.wait_ge(s_gat, 16 * KT * e)
                dve.tensor_copy(gate[:, k, :].unsqueeze(2), xg[:, :, bass.ds(D + e, 1)]).then_inc(s_gate, 1)

            def expert(g, k):
                e = GS * g + k
                numbers(e + 1, 1 - k)
                spread(e + 2)
                gates(e + 1, 1 - k)
                dve.wait_ge(s_ybfree, e + 1)
                dve.tensor_copy(idx_add[:], idx[:, k, :]).then_inc(s_idadd, 1)
                for j in range(KT):
                    dve.wait_ge(s_dmm, KT * e + (j + 1))
                    dve.tensor_scalar(yb[:, j, :], ps[:, 4 + j % 2, 0:D], gate[:, k, j:j + 1], None, ALU.mult).then_inc(s_y, 1)

            dve.sem_inc(s_y, 2)
            dve.wait_ge(s_iotas, 1)
            spread(0)
            numbers(0, 0)
            spread(1)
            gates(0, 0, True)
            with dve.Fori(0, G - 1) as g:
                for k in range(GS):
                    expert(g, k)

            def moments(first, row, count):
                if first:
                    dve.wait_ge(s_fmv, first)
                for t in range(count):
                    dve.bn_stats(fst[:, t, :], row(t)).then_inc(s_fst, 1)
                for t in range(count):
                    dve.wait_ge(s_fst, first + t + 1)
                    dve.bn_aggr(fmv[:, first + t, :], fst[:, t, :]).then_inc(s_fmv, 1)

            def block_moments(b):
                dve.wait_ge(s_yin[b], 16)
                moments(b * TB, lambda t: h_all[:, b * TB + t, 0:D], TB)

            def late_sum(e, j, out_):
                bank = (4, 5, 2, 3)[j] if e == E - 1 else 4 + j % 2
                dve.wait_ge(s_dmm, KT * e + (j + 1))
                dve.scalar_tensor_tensor(out=out_[:, j, :], in0=ps[:, bank, 0:D], scalar=gate[:, e - LATE, j:j + 1],
                                         in1=y_late[:, j, :], op0=ALU.mult, op1=ALU.add).then_inc(s_y, 1)

            numbers(E - 1, 1)
            gates(E - 1, 1)
            dve.wait_ge(s_add, 16 * KT * LATE)
            dve.wait_ge(s_ylate, 16 * KT)
            late_sum(LATE, 0, yb)
            for j in range(1, KT):
                late_sum(LATE, j, yb)
                block_moments(j - 1)
            block_moments(KT - 1)
            for b in range(KT, NB):
                block_moments(b)
            dve.wait_ge(s_y, KT * (LATE + 1) + 2)
            moments(NT, lambda t: yb[:, t, :], KT)
            for tile in range(NT - 2 * TB, NT):
                dve.wait_ge(s_frs, tile + 1)
                dve.tensor_scalar(h_all[:, tile, 0:D], h_all[:, tile, 0:D], fmv[:, tile, 0:1], frs[:, tile:tile + 1],
                                  ALU.subtract, ALU.mult).then_inc(s_fin_last, 1)
            dve.wait_ge(s_ylate, 2 * 16 * KT)
            for j in range(KT):
                late_sum(E - 1, j, y_last)
            dve.wait_ge(s_y, KT * E + 2)
            moments(NT + KT, lambda t: y_last[:, t, :], KT)

        @block.scalar
        def _(act):
            def keys(i, j, kind):
                if not has(kind, j, 0):
                    return
                act.wait_ge(s_kx, 4 * i + (j + 3))
                if kind != "first" or j >= 2:
                    act.wait_ge(s_key, 4 * i + (j - 1))
                act.activation(kneg[:, j % 2, :], kx[:, j % 2, :], ACT.Relu, scale=-1.0).then_inc(s_kneg, 1)
                act.wait_ge(s_kneg, 4 * i + (j + 1))
                act.activation(kexp[:, j % 2, :], kneg[:, j % 2, :], ACT.Exp, scale=-1.0).then_inc(s_kexp, 1)

            pair_steps(act, keys)

            def queries(n, m):
                act.wait_ge(s_qmm, C * n + (m + 1))
                act.activation(qrel[:, m, :], ps[:, m, :], ACT.Relu, bias=bq_s[:, m:m + 1])
                act.activation(qexp[:, m, :], ps[:, m, :], ACT.Exp, bias=bq_s[:, m:m + 1]).then_inc(s_qread, 1)

            def tokens(n, t, kind):
                tile = TB * (n - HALF) + t
                first = 0 if has_row(kind, t, 0) else C
                last = 2 * C if has_row(kind, t, 5) else C
                if first < last:
                    act.wait_ge(s_turnmm, tile + 1)
                    act.copy(turned[:, t, first:last, :].rearrange("p c k -> p (c k)"), ps[:, 4, first * P:last * P]).then_inc(s_turned, 1)
                if has_row(kind, t, 4):
                    act.wait_ge(s_shift2, tile - 3)
                    act.wait_ge(s_x1out[t], 32 * (n - HALF))
                    act.activation(x1[:, t, :], us[:, t, :], ACT.Identity, bias=shift2[:, (t - 1) % TB:(t - 1) % TB + 1],
                                   scale=rstd[:, (t - 1) % TB, 1:2]).then_inc(s_x1, 1)
                if prefetches(kind) and t < C:
                    act.wait_ge(s_q, 2 * n + 2)
                    queries(n + 1, t)

            act.sem_inc(s_turned, 1)
            act.sem_inc(s_x1, TB)
            act.wait_ge(s_wts, 16 * 9)
            for m in range(C):
                queries(0, m)
            tile_steps(act, tokens)

            act.wait_ge(s_soft, 2)
            act.activation(lg[:], prob[:], ACT.Exp).then_inc(s_exp, 1)
            act.copy(iotas, cs[:, C_IOTA:C_IOTA + P].unsqueeze(2).to_broadcast([P, P, NT])).then_inc(s_iotas, 1)
            act.activation(spare[:], cs[:, C_PART:C_PART + 1], ACT.Silu).then_inc(s_spare, 1)

            def turn(e):
                act.wait_ge(s_xtmm, e + 1)
                for c in range(C):
                    act.copy(xgt[:, c, :], ps[:, 2 + c, :]).then_inc(s_xt, 1)

            def up(g, e, f):
                width = P if f < FT - 1 else FR
                stand(act, s_umm, FT * e + (f + 1))
                act.activation(mid[0:width, f, :], ps[0:width, f % 2, :], ACT.Silu,
                               bias=bup_s[0:width, bass.ds(g, 1), f:f + 1].rearrange("p a f -> p (a f)")).then_inc(s_mid, 1)

            def expert(g, k, last):
                e = GS * g + k
                for f in range(FT):
                    up(g, e, f)
                if not last:
                    turn(e + 1)

            act.sem_inc(s_mid, 2)
            turn(0)
            with act.Fori(0, G - 1) as g:
                for k in range(GS):
                    expert(g, k, False)

            def normed(tile, out_, in_):
                act.wait_ge(s_fnm, tile + 1)
                act.activation(out_, in_, ACT.Identity, bias=fnm[:, tile:tile + 1], scale=frs[:, tile:tile + 1]).then_inc(s_fin, 1)

            def normed_row(tile):
                normed(tile, h_all[:, tile, 0:D], h_all[:, tile, 0:D])

            expert(G - 1, 0, False)
            for tile in range(2 * TB):
                normed_row(tile)
            for f in range(FT):
                up(G - 1, E - 1, f)
                for tile in range(2 * TB + 2 * f, 2 * TB + 2 * f + 2):
                    normed_row(tile)
            for tile in range(2 * TB + 2 * FT, NT - 2 * TB):
                normed_row(tile)
            for j in range(KT):
                normed(NT + j, o_late[:, 0, j, :], yb[:, j, :])
            for j in range(KT):
                normed(NT + KT + j, o_late[:, 1, j, :], y_last[:, j, :])

        @block.gpsimd
        def _(pool):
            def tokens(n, t, kind):
                tile = TB * (n - HALF) + t
                first = 0 if has_row(kind, t, 1) else 1
                last = 2 if has_row(kind, t, 3) else 1
                if first < last:
                    if last == 2:
                        pool.wait_ge(s_mv2, tile - 2)
                    if first == 0:
                        pool.wait_ge(s_mv, tile)
                    pool.tensor_tensor(ve[:, t, first:last], mv[:, t, first:last, 1], cs[:, C_EPS:C_EPS + last - first],
                                       ALU.add).then_inc(s_ve, 1)
                    if last == 2:
                        pool.tensor_tensor(nm[:, t:t + 1], mv[:, t, 1, 0:1], cs[:, C_NEG:C_NEG + 1], ALU.mult).then_inc(s_nm, 1)
                    pool.wait_ge(s_ve, tile)
                    pool.tensor_tensor(rstd[:, t, first:last], ve[:, t, first:last], cs[:, C_HALF:C_HALF + last - first],
                                       ALU.pow).then_inc(s_rs, 1)
                if last == 2:
                    pool.wait_ge(s_nm, tile - 2)
                    pool.wait_ge(s_rs, tile)
                    pool.tensor_tensor(shift2[:, t:t + 1], nm[:, t:t + 1], rstd[:, t, 1:2], ALU.mult).then_inc(s_shift2, 1)

            pool.wait_ge(s_rows, 16)
            for pair in range(NT // 2 - 4, NT // 2):
                tiles = h_all[:, 2 * pair:2 * pair + 2, 0:D]
                pool.wait_ge(s_khmm, pair + 1)
                pool.tensor_tensor(tiles, tiles, tiles, ALU.add).then_inc(s_x2late, 1)
                pool.wait_ge(s_x2late, 2 * (pair - NT // 2 + 4) + 1)
                pool.tensor_tensor(tiles, tiles, rw[:, R_BETA:R_BETA + D].unsqueeze(1).to_broadcast([P, 2, D]),
                                   ALU.add).then_inc(s_x2late, 1)
            pool.wait_ge(s_wts, 16 * 9)
            tile_steps(pool, tokens)

            for t in range(TB):
                pool.wait_ge(s_x1out[t], 32 * NB + 32)
            pool.wait_ge(s_probout, 16)

            def gather(e, k, slot_used):
                if slot_used:
                    pool.wait_ge(s_xtmm, e)
                    pool.wait_ge(s_gate, e)
                stand(pool, s_idx, e + 1)
                for j in range(KT):
                    pool.indirect_dma_start(out=xg[:, j, :], out_offset=None, in_=table[:, :],
                                            in_offset=bass.IndirectOffsetOnAxis(ap=idx[:, k, j:j + 1], axis=0)).then_inc(s_gat if slot_used else s_first[j], 16)

            def add_rows(e):
                pool.wait_ge(s_y, KT * e + (KT + 2))
                stand(pool, s_idadd, e + 1)
                for j in range(KT):
                    pool.indirect_dma_start(out=ysum[:, :], out_offset=bass.IndirectOffsetOnAxis(ap=idx_add[:, j:j + 1], axis=0),
                                            in_=yb[:, j, :], in_offset=None, compute_op=ALU.add).then_inc(s_add, 16)

            pool.sem_inc(s_ybfree, 1)
            gather(0, 0, False)
            gather(1, 1, True)
            with pool.Fori(0, G - 1) as g:
                for k in range(GS):
                    e = GS * g + k
                    add_rows(e)
                    gather(e + 2, k, True)
                    pool.wait_ge(s_add, 16 * KT * e + 16 * KT)
                    pool.sem_inc(s_ybfree, 1)

            def factors(first, count):
                at = slice(first, first + count)
                pool.wait_ge(s_fmv, first + count)
                pool.tensor_tensor(fve[:, at], fmv[:, at, 1], cs[:, C_EPS:C_EPS + count], ALU.add).then_inc(s_fve, count)
                pool.wait_ge(s_fve, first + count)
                pool.tensor_tensor(frs[:, at], fve[:, at], cs[:, C_HALF:C_HALF + count], ALU.pow).then_inc(s_frs, count)
                pool.wait_ge(s_frs, first + count)
                pool.tensor_tensor(fmr[:, at], fmv[:, at, 0], frs[:, at], ALU.mult).then_inc(s_fmr, count)
                pool.wait_ge(s_fmr, first + count)
                pool.tensor_tensor(fnm[:, at], fmr[:, at], cs[:, C_NEG:C_NEG + count], ALU.mult).then_inc(s_fnm, count)

            def late_rows(k):
                for j in range(KT):
                    pool.indirect_dma_start(out=y_late[:, j, :], out_offset=None, in_=ysum[:, :],
                                            in_offset=bass.IndirectOffsetOnAxis(ap=idx[:, k, j:j + 1], axis=0)).then_inc(s_ylate, 16)

            pool.wait_ge(s_ybfree, LATE + 1)
            late_rows(0)
            for b in range(KT):
                factors(b * TB, TB)
            for b in range(NB):
                pool.wait_ge(s_yin[b], 16)
            pool.wait_ge(s_y, KT * (LATE + 1) + 2)
            for j in range(KT):
                pool.indirect_dma_start(out=ysum[:, :], out_offset=bass.IndirectOffsetOnAxis(ap=idx[:, 0, j:j + 1], axis=0),
                                        in_=yb[:, j, :], in_offset=None).then_inc(s_into, 16)
            factors(KT * TB, 2 * TB)
            factors(KT * TB + 2 * TB, 2 * TB)
            pool.wait_ge(s_into, 16 * KT)
            late_rows(1)
            factors(NT, KT)

            def late_out(k, j):
                pool.wait_ge(s_fin, NT - 2 * TB + KT * k + j + 1)
                pool.indirect_dma_start(out=out[:, :], out_offset=bass.IndirectOffsetOnAxis(ap=idx[:, k, j:j + 1], axis=0),
                                        in_=o_late[:, k, j, :], in_offset=None).then_inc(s_late, 16)

            pool.wait_ge(s_out, 16 * NB)
            for j in range(KT):
                late_out(0, j)
            factors(NT + KT, KT)
            pool.wait_ge(s_late, 16 * KT)
            for j in range(KT):
                late_out(1, j)


def kernel(L0_attn_H, L0_attn_W_qkv, L0_attn_b_qkv, L0_attn_W_proj, L0_attn_b_proj, L0_attn_gamma, L0_attn_beta,
           L0_ffn_Wr, L0_ffn_br, L0_ffn_W_up, L0_ffn_b_up, L0_ffn_W_down, L0_ffn_b_down):
    import concourse.bacc as bacc
    from concourse.bass_utils import run_bass_kernel_spmd

    x = np.asarray(L0_attn_H)[0]
    bqkv = np.asarray(L0_attn_b_qkv)
    rows = np.concatenate([bqkv[D:2 * D], L0_attn_b_proj, L0_attn_gamma, L0_attn_beta, L0_ffn_br])
    bup = np.zeros((G, FT * P), np.float32)
    bup[:, :F] = L0_ffn_b_up
    cst, steps = constants()
    xs = x.reshape(PER, 2, P, D).transpose(1, 0, 2, 3).reshape(N, D)
    xq = x.reshape(2, P, PER, D).transpose(0, 2, 1, 3).reshape(N, D)
    ins = {
        "x": xs,
        "xt": xs.T,
        "xtq": xq.T,
        "wqkv": np.asarray(L0_attn_W_qkv).T,
        "bq": bqkv[:D].reshape(C, P).T,
        "bv": bqkv[2 * D:].reshape(1, D),
        "wp": np.asarray(L0_attn_W_proj).T,
        "rows": np.broadcast_to(rows, (P, R_ALL)),
        "wr": np.asarray(L0_ffn_Wr),
        "wup": np.asarray(L0_ffn_W_up),
        "bup": bup.reshape(G, FT, P).transpose(2, 0, 1),
        "wdn": np.concatenate([L0_ffn_W_down, np.asarray(L0_ffn_b_down)[:, None, :]], axis=1),
        "cst": cst,
        "steps": steps,
    }
    nc = bacc.Bacc("TRN2", target_bir_lowering=False, num_devices=1)
    arrays, args = {}, []
    for name, a in ins.items():
        a = np.ascontiguousarray(a)
        arrays[name] = a
        args.append(nc.dram_tensor(name, a.shape, mybir.dt.from_np(a.dtype), kind="ExternalInput").ap())
    args.append(nc.dram_tensor("out", (N, D), F32, kind="ExternalOutput").ap())
    build(nc, *args)
    r = run_bass_kernel_spmd(nc, [arrays], core_ids=[0])
    return r.results[0]["out"].reshape(2, PER, P, D).transpose(1, 0, 2, 3).reshape(1, N, D)
```
